# Optimizing a Trainium2 kernel written in Bass

```python
import numpy as np
import jax
import jax.numpy as jnp

def _softmax(x, axis=-1):
    return jax.nn.softmax(x, axis=axis)

def _gelu(x):
    return jax.nn.gelu(x, approximate=True)

def _silu(x):
    return jax.nn.silu(x)

def _sigmoid(x):
    return jax.nn.sigmoid(x)

def _layernorm(x, axis=-1, eps=1e-05):
    m = jnp.mean(x, axis=axis, keepdims=True)
    v = jnp.var(x, axis=axis, keepdims=True)
    return (x - m) / jnp.sqrt(v + eps)

def _scatter_add(tgt, idx, src, axis=0):
    return tgt.at[idx].add(src)

def _segment_sum(src, seg, n):
    return jax.ops.segment_sum(src, seg, n)
kernel_name = 'mk_prb_d1_jaxref_r4_2d5e0e'

def setup_inputs(seed: int=0):
    np.random.seed(seed)
    _w = jnp.asarray

    def _L0_attn_setup():
        import jax, jax.numpy as jnp
        import numpy as np
        B, S, E, H, L = (2, 512, 512, 16, 128)
        HD = E // H

        def _reference_tuple_inner(x, Wq, Wdkv, Wuk, Wuv, ln_g, ln_b, Wo_h, Wo, bo):
            Bx, Sx, Ex = x.shape
            xh = x.reshape(Bx, Sx, H, HD).transpose(0, 2, 1, 3)
            c = jnp.einsum('bhsd,hld->bhsl', xh, Wdkv)
            mu = c.mean(-1, keepdims=True)
            var = c.var(-1, keepdims=True)
            c = (c - mu) * jax.lax.rsqrt(var + 1e-05)
            c = c * ln_g[None, :, None, :] + ln_b[None, :, None, :]
            absorbed = jnp.einsum('hij,hlj->hil', Wq, Wuk)
            q_lat = jnp.einsum('bhsd,hdl->bhsl', xh, absorbed)
            scores = jnp.einsum('bhsl,bhtl->bhst', q_lat, c)
            scores = scores * (1.0 / np.sqrt(L).astype(np.float32))
            mask = jnp.tril(jnp.ones((Sx, Sx), dtype=bool))
            scores = jnp.where(mask, scores, -jnp.inf)
            w = jax.nn.softmax(scores, axis=-1)
            v = jnp.einsum('bhsl,hld->bhsd', c, Wuv)
            oh = jnp.einsum('bhst,bhtd->bhsd', w, v)
            oh = jnp.einsum('bhsd,hed->bhse', oh, Wo_h)
            o = oh.transpose(0, 2, 1, 3).reshape(Bx, Sx, Ex)
            out = o @ Wo.T + bo
            return (out, c)
        key = jax.random.key(seed)
        ks = jax.random.split(key, 8)
        sd = 0.02
        return {'x': jax.random.normal(ks[0], (B, S, E), jnp.float32), 'Wq': jax.random.normal(ks[1], (H, HD, HD), jnp.float32) * sd, 'Wdkv': jax.random.normal(ks[2], (H, L, HD), jnp.float32) * sd, 'Wuk': jax.random.normal(ks[3], (H, L, HD), jnp.float32) * sd, 'Wuv': jax.random.normal(ks[4], (H, L, HD), jnp.float32) * sd, 'ln_g': jnp.ones((H, L), jnp.float32), 'ln_b': jnp.zeros((H, L), jnp.float32), 'Wo_h': jax.random.normal(ks[5], (H, HD, HD), jnp.float32) * sd, 'Wo': jax.random.normal(ks[6], (E, E), jnp.float32) * sd, 'bo': jnp.zeros((E,), jnp.float32)}
    _L0_attn_in = _L0_attn_setup()

    def _L0_ffn_setup():
        import jax, jax.numpy as jnp
        import numpy as np
        N, S, D = (8, 512, 512)
        O = 512
        E = 8
        K = 2
        key = jax.random.key(seed)
        ks = jax.random.split(key, 5)
        scale_in = 1.0 / np.sqrt(D)
        x = jax.random.normal(ks[0], (N, S, D), dtype=jnp.float32)
        gate_w = jax.random.uniform(ks[1], (D, E), dtype=jnp.float32, minval=-scale_in, maxval=scale_in)
        gate_b = jax.random.uniform(ks[2], (E,), dtype=jnp.float32, minval=-scale_in, maxval=scale_in)
        expert_w = jax.random.uniform(ks[3], (E, D, O), dtype=jnp.float32, minval=-scale_in, maxval=scale_in)
        expert_b = jax.random.uniform(ks[4], (E, O), dtype=jnp.float32, minval=-scale_in, maxval=scale_in)
        return {'x': x, 'gate_w': gate_w, 'gate_b': gate_b, 'expert_w': expert_w, 'expert_b': expert_b}
    _L0_ffn_in = _L0_ffn_setup()
    _d = {'L0_attn_x': _L0_attn_in['x'], 'L0_attn_Wq': _L0_attn_in['Wq'], 'L0_attn_Wdkv': _L0_attn_in['Wdkv'], 'L0_attn_Wuk': _L0_attn_in['Wuk'], 'L0_attn_Wuv': _L0_attn_in['Wuv'], 'L0_attn_ln_g': _L0_attn_in['ln_g'], 'L0_attn_ln_b': _L0_attn_in['ln_b'], 'L0_attn_Wo_h': _L0_attn_in['Wo_h'], 'L0_attn_Wo': _L0_attn_in['Wo'], 'L0_attn_bo': _L0_attn_in['bo'], 'L0_ffn_gate_w': _L0_ffn_in['gate_w'], 'L0_ffn_gate_b': _L0_ffn_in['gate_b'], 'L0_ffn_expert_w': _L0_ffn_in['expert_w'], 'L0_ffn_expert_b': _L0_ffn_in['expert_b']}
    _x0 = _d['L0_attn_x']
    _d['L0_attn_x'] = jax.random.normal(jax.random.fold_in(jax.random.key(seed), 1), (2, 2048, 512), dtype=_x0.dtype)
    del _x0
    return _d

def reference(L0_attn_x, L0_attn_Wq, L0_attn_Wdkv, L0_attn_Wuk, L0_attn_Wuv, L0_attn_ln_g, L0_attn_ln_b, L0_attn_Wo_h, L0_attn_Wo, L0_attn_bo, L0_ffn_gate_w, L0_ffn_gate_b, L0_ffn_expert_w, L0_ffn_expert_b):

    def _L0_attn_ref(x, Wq, Wdkv, Wuk, Wuv, ln_g, ln_b, Wo_h, Wo, bo):
        import jax, jax.numpy as jnp
        import numpy as np
        B, S, E, H, L = (2, 512, 512, 16, 128)
        HD = E // H

        def _reference_tuple_inner(x, Wq, Wdkv, Wuk, Wuv, ln_g, ln_b, Wo_h, Wo, bo):
            Bx, Sx, Ex = x.shape
            xh = x.reshape(Bx, Sx, H, HD).transpose(0, 2, 1, 3)
            c = jnp.einsum('bhsd,hld->bhsl', xh, Wdkv)
            mu = c.mean(-1, keepdims=True)
            var = c.var(-1, keepdims=True)
            c = (c - mu) * jax.lax.rsqrt(var + 1e-05)
            c = c * ln_g[None, :, None, :] + ln_b[None, :, None, :]
            absorbed = jnp.einsum('hij,hlj->hil', Wq, Wuk)
            q_lat = jnp.einsum('bhsd,hdl->bhsl', xh, absorbed)
            scores = jnp.einsum('bhsl,bhtl->bhst', q_lat, c)
            scores = scores * (1.0 / np.sqrt(L).astype(np.float32))
            mask = jnp.tril(jnp.ones((Sx, Sx), dtype=bool))
            scores = jnp.where(mask, scores, -jnp.inf)
            w = jax.nn.softmax(scores, axis=-1)
            v = jnp.einsum('bhsl,hld->bhsd', c, Wuv)
            oh = jnp.einsum('bhst,bhtd->bhsd', w, v)
            oh = jnp.einsum('bhsd,hed->bhse', oh, Wo_h)
            o = oh.transpose(0, 2, 1, 3).reshape(Bx, Sx, Ex)
            out = o @ Wo.T + bo
            return (out, c)
        return _reference_tuple_inner(x, Wq, Wdkv, Wuk, Wuv, ln_g, ln_b, Wo_h, Wo, bo)[0]

    def _L0_ffn_ref(x, gate_w, gate_b, expert_w, expert_b):
        import jax, jax.numpy as jnp
        import numpy as np
        N, S, D = (8, 512, 512)
        O = 512
        E = 8
        K = 2
        gate_logits = jnp.einsum('nsd,de->nse', x, gate_w) + gate_b
        _, top_idx = jax.lax.top_k(gate_logits, K)
        all_out = jax.nn.relu(jnp.einsum('nsd,edo->nseo', x, expert_w) + expert_b)
        sel = jnp.take_along_axis(all_out, top_idx[..., None], axis=2)
        return sel.mean(axis=2)
    x = L0_attn_x
    xn = _layernorm(x, axis=-1)
    x = x + _L0_attn_ref(xn, L0_attn_Wq, L0_attn_Wdkv, L0_attn_Wuk, L0_attn_Wuv, L0_attn_ln_g, L0_attn_ln_b, L0_attn_Wo_h, L0_attn_Wo, L0_attn_bo) + _L0_ffn_ref(xn, L0_ffn_gate_w, L0_ffn_gate_b, L0_ffn_expert_w, L0_ffn_expert_b)
    return x

_drawn_inputs = setup_inputs


def setup_inputs(seed=0):
    import zlib

    import numpy as np

    out = dict(_drawn_inputs(seed))
    spreads = {'L0_attn_ln_g': (1.0, 0.6), 'L0_attn_ln_b': (0.0, 0.8), 'L0_attn_bo': (0.0, 0.456)}
    factors = {'L0_attn_Wq': 8.0,
     'L0_attn_Wdkv': 8.0,
     'L0_attn_Wuk': 8.0,
     'L0_attn_Wuv': 8.0,
     'L0_attn_Wo_h': 8.0,
     'L0_attn_Wo': 8.0,
     'L0_ffn_expert_b': 25.187,
     'L0_ffn_gate_b': 6.381}
    for name, (base, spread) in spreads.items():
        noise = np.random.default_rng([zlib.crc32(name.encode()), seed]).standard_normal(out[name].shape)
        drawn = base * np.exp(spread * noise) if base else spread * noise
        out[name] = jnp.asarray(drawn.astype(out[name].dtype))
    for name, factor in factors.items():
        out[name] = (out[name] * factor).astype(out[name].dtype)
    return out
```

```python
import concourse.bass as bass
from concourse import mybir
from contextlib import ExitStack


def layer_kernel(nc, x, Wq, Wdkv, Wuk, Wuv, ln_g, ln_b, Wo_h, Wo, bo,
                 gate_w, gate_b, expert_w, expert_b, out):
    f32, f16, u32 = mybir.dt.float32, mybir.dt.float16, mybir.dt.uint32
    ALU, ACT, AX = mybir.AluOpType, mybir.ActivationFunctionType, mybir.AxisListType.X
    ds = bass.ds

    B, S, E = x.shape
    H, L, HD = Wdkv.shape
    NE = gate_w.shape[1]
    P = 128
    KB = E // P
    HK = P // HD
    CH = 512
    CT = CH // P
    NC = S // CH
    ST = S // P
    BH = B * H
    V1 = HD + 1
    SCALE = 1.0 / float(L) ** 0.5
    WS = 256.0
    MS = 64.0
    LOWEST = -3.0e38
    FAR = 32768.0
    EPS = 1e-5

    q_dram = nc.dram_tensor("q_pieces", (2, BH * HD, S), f16, kind="Internal").ap()
    k_dram = nc.dram_tensor("k_pieces", (2, BH * HD, S), f16, kind="Internal").ap()
    v_dram = nc.dram_tensor("v_rows", (BH, P, ST, V1), f32, kind="Internal").ap()
    xt_dram = nc.dram_tensor("xn_t_pieces", (B * ST, P, KB * 2 * P), f16, kind="Internal").ap()

    ctx = ExitStack()
    with ctx:
        def sb(name, shape, dt):
            return ctx.enter_context(nc.sbuf_tensor(name, shape, dt))

        def sem(name):
            return ctx.enter_context(nc.semaphore(name))

        arena1 = sb("arena1", [P, 16384], f32)
        arena2 = sb("arena2", [P, 10304], f32)
        w_hi = sb("w_hi", [P, NE, KB * E], f16)
        w_lo = sb("w_lo", [P, NE, KB * E], f16)
        eb_bc = sb("eb_bc", [P, NE, E], f32)
        comb = sb("comb", [P, KB, E], f32)
        bo_bc = sb("bo_bc", [P, E], f32)
        bv_bc = sb("bv_bc", [P, E], f32)
        ident = sb("ident", [P, P], f32)
        ident16 = sb("ident16", [P, P], f16)
        tri = sb("tri", [P, P], f32)
        head_of = sb("head_of", [P, KB, H], f32)
        of_head = sb("of_head", [H, KB * P], f32)
        bk = sb("bk", [P, KB], f32)
        gw_hl = sb("gw_hl", [P, 2, KB, NE], f16)
        gw_raw = sb("gw_raw", [P, KB, NE], f32)
        gb_bc = sb("gb_bc", [P, NE], f32)
        eps = sb("eps", [P, 1], f32)
        ws_col = sb("ws_col", [P, 1], f32)
        deny = sb("deny", [P, P], f16)
        later = sb("later", [P, 2, 2 * P], f16)
        iota = sb("iota", [P, NE], f32)
        route = sb("route", [P, ST, B, NE], f32)

        def carve(arena):
            at = [0]

            def take(n, dt=f32):
                w = n if dt == f32 else n // 2
                a = arena[:, at[0]:at[0] + w]
                at[0] += w
                assert at[0] <= arena.shape[1], at[0]
                return a if dt == f32 else a.bitcast(dt)
            return take

        t0 = carve(arena1)
        wdkv = t0(H * HD)
        wuk = t0(H * HD)
        wuv = t0(H * HD)
        wc = t0(H * HD)
        gwuk = t0(H * HD)
        gwuv = t0(H * HD)
        g_t = t0(H)
        b_t = t0(H)
        center = t0(P)
        bdo = t0(KB * P).rearrange("p (k c) -> p k c", k=KB)
        wo_raw = t0(4 * E).rearrange("p (n c) -> p n c", n=4)
        wo_t = t0(KB * E).rearrange("p (k c) -> p k c", k=KB)
        tA = carve(arena2)
        xhl = tA(CT * KB * 2 * P, f16).rearrange("p (t k z c) -> p t k z c", t=CT, k=KB, z=2)
        q_hi, q_lo, k_hi, k_lo = (tA(KB * CH, f16).rearrange("p (k s) -> p k s", k=KB) for _ in range(4))
        v_st = tA(CT * H * V1).rearrange("p (h t f) -> p h t f", t=CT, h=H)
        stage = tA(KB * E)
        tA = carve(arena1)
        tA(6 * CT * E)
        bdq, bdk, bdg, bdv = (tA(KB * P).rearrange("p (k c) -> p k c", k=KB) for _ in range(4))
        small = tA(512)
        tA = carve(arena1)
        x_in = [tA(CT * E).rearrange("p (t c) -> p t c", t=CT) for _ in range(2)]
        xn = tA(CT * E).rearrange("p (t c) -> p t c", t=CT)
        x_t = tA(KB * CH).rearrange("p (k s) -> p k s", k=KB)
        prod = tA(KB * CH).rearrange("p (k s) -> p k s", k=KB)
        xr = tA(KB * CH).rearrange("p (k s) -> p k s", k=KB)
        rs_row = small[0:H, 0:CH]
        sd_buf = sb("sd_row", [H, CH], f32)
        stats = sb("stats", [P, CT, 6], f32)
        mv = sb("mv", [P, CT, 2], f32)
        sd4 = sb("sd4", [P, CT], f32)
        rs4 = sb("rs4", [P, CT], f32)
        lg = sb("lg", [P, CT, NE], f32)
        top8 = sb("top8", [P, CT, 8], f32)
        idx8 = sb("idx8", [P, CT, 8], u32)
        idxf = sb("idxf", [P, CT, 8], f32)
        eq0 = sb("eq0", [P, CT, NE], f32)
        eq1 = sb("eq1", [P, CT, NE], f32)
        attn = arena1[:, :].rearrange("p (t g d) -> p t g d", t=ST, g=BH)
        tB = carve(arena2)
        probs = [tB(2 * CH) for _ in range(4)]
        q_st = [tB(S, f16) for _ in range(2)]
        k_st = [tB(S, f16) for _ in range(2)]
        v_sb = [tB(ST * V1).rearrange("p (j f) -> p j f", j=ST) for _ in range(2)]
        ot = [tB(CH) for _ in range(2)]
        PMS = 6
        pm = sb("pm", [P, NC, CT, PMS], f32)
        mx = sb("mx", [P, NC, CT], f32)
        mx16 = sb("mx16", [P, NC, CT], f16)
        half_b = sb("half_b", [P, CT, V1], f32)
        whole = sb("whole", [P, CT, V1], f32)
        rden = sb("rden", [P, CT, 1], f32)
        tC = carve(arena2)
        xc_t = [tC(KB * 2 * P, f16).rearrange("p (k z c) -> p k z c", k=KB, z=2) for _ in range(B)]
        xc = [tC(E) for _ in range(B)]
        o_in = [tC(E) for _ in range(B)]
        o_t = [tC(E).rearrange("p (k c) -> p k c", k=KB) for _ in range(B)]
        proj = [tC(E) for _ in range(B)]
        acc = [tC(E) for _ in range(B)]
        NZ = 4
        z_sb = [tC(E) for _ in range(NZ)]
        r_sb = [tC(E) for _ in range(NZ)]
        w_t = sb("w_t", [P, B, NE], f32)
        junk = bv_bc[:, :].rearrange("p (r c) -> p r c", r=CT)

        PS = ctx.enter_context(nc.psum_tensor("PS", [P, 8, CH], f32))

        s = {n: sem(n) for n in (
            "w_in wqo_in g_in zeroed consts wc_ps wc_done gw_done fold_ps fold_done bk_ps bk_done bv_ps bv_done "
            "wot_ps wot_done comb_ps comb_done gates_done dve0 "
            "x_in0 x_in1 stage_in stage_free pool_link sd4_done xn_done tp_ps xt_done xh_done xl_done y_ps prod_done "
            "var_ps sd_done rs_done rb_ps xr_done q_ps qh_done ql_done k_ps kh_done kl_done vv_ps v_done lg_ps lg_done "
            "stored dveA mv_done "
            "ld0 ld1 b_zero s1_ps s1_done mx_done m_ps m_done s2_ps exp_done pv_done ot_done tr_ps norm_done dveB "
            "xt_in0 xt_in1 xc_in0 xc_in1 o_done otp_ps otc_done proj_ps proj_done z_ps z_done r_done acc_done out_done0 out_done1 poolC"
        ).split()}

        def linker(engine, semaphore, base=0):
            n = [0]

            def link(ins):
                n[0] += 1
                ins.then_inc(semaphore, 1)
                engine.wait_ge(semaphore, count(base + n[0]))
            return link, n

        def count(n):
            return n + 1

        def since(base, k):
            return base + max(k, 0)

        block = ctx.enter_context(nc.Block())

        x_v = x.rearrange("b (g p) d -> b p g d", p=P)
        q_v = q_dram.rearrange("z (b k r) s -> z b r k s", b=B, k=KB)
        k_v = k_dram.rearrange("z (b k r) s -> z b r k s", b=B, k=KB)
        v_v = v_dram.rearrange("(b h) r j f -> b r h (j f)", b=B)
        xt_v = xt_dram.rearrange("(b g) r f -> b r g f", b=B)
        ew_v = expert_w.rearrange("e (k p) o -> p e k o", p=P)
        out_v = out.rearrange("b (t p) d -> b t p d", p=P)
        xc_v = x.rearrange("b (t p) d -> b t p d", p=P)

        STORES_A = 6
        A_LINKS = 5

        def head_units():
            units = []
            for c in range(NC):
                d0 = CT * c
                if c == 0:
                    own = [(c, 0, (CH, CH), CH, True), (c, 2, (2 * P, P), 2 * P, True)]
                    units += own
                    continue
                full = [(c, j, (CH, CH), CH, False) for j in range(0, d0, 2)]
                diag = [(c, d0, (CH, CH - P), CH, True), (c, d0 + 2, (2 * P, P), 2 * P, True)]
                units += full[:1] + diag + full[1:]
            return units

        UNITS = head_units()
        NU = len(UNITS)
        LAST = {max(k for k, un in enumerate(UNITS) if un[0] == c): c for c in range(NC)}
        FIRST = {min(k for k, un in enumerate(UNITS) if un[0] == c): c for c in range(NC)}
        PIECES = [(i, p, min(CH, P * (i + 1) - CH * p)) for i in range(ST) for p in range(i // CT + 1)]
        NP_ = len(PIECES)
        PV_LAG = 2
        S1_FROM = 5
        EARLY = NP_ - 2 * S1_FROM

        def slot_pieces(k):
            if k < S1_FROM:
                return [(0, EARLY + 2 * k), (0, EARLY + 2 * k + 1)]
            return [(1, 2 * (k - S1_FROM)), (1, 2 * (k - S1_FROM) + 1)]

        CHUNK_END = {max(n for n, pc in enumerate(PIECES) if pc[0] // CT == c): c for c in range(NC)}

        def slot_max_rows(k):
            done = slot_pieces(k - 1) if k else []
            return [(ahead, CHUNK_END[n]) for ahead, n in done if n in CHUNK_END]

        assert 2 * (NU - S1_FROM) == EARLY and (NP_ - 1) // 2 * 2 + 1 == NP_ - 1

        @block.sync
        def _(sp):
            for semaphore in s.values():
                sp.sem_inc(semaphore, 1)
            sp.dma_start(wdkv.rearrange("p (h d) -> p h d", h=H), Wdkv.rearrange("h l d -> l h d")).then_inc(s["w_in"], 16)
            sp.dma_start(wuk.rearrange("p (h d) -> p h d", h=H), Wuk.rearrange("h l d -> l h d")).then_inc(s["w_in"], 16)
            sp.dma_start(wuv.rearrange("p (h d) -> p h d", h=H), Wuv.rearrange("h l d -> l h d")).then_inc(s["w_in"], 16)
            sp.dma_start(wo_raw, Wo.rearrange("(n p) c -> p n c", p=P)).then_inc(s["w_in"], 16)
            sp.wait_ge(s["zeroed"], count(1))
            for j in range(HK):
                r = slice(HD * j, HD * (j + 1))
                sp.dma_start(bdq[r, :, r], Wq.rearrange("(k j) i o -> j i k o", j=HK)[j]).then_inc(s["wqo_in"], 16)
                sp.dma_start(bdo[r, :, r], Wo_h.rearrange("(k j) e d -> j e k d", j=HK)[j]).then_inc(s["wqo_in"], 16)
            sp.wait_ge(s["comb_done"], count(KB))
            with sp.Fori(0, NC) as i:
                for u in range(B):
                    n = i * B + u
                    sp.wait_ge(s["xn_done"], count(n * CT))
                    sp.dma_start(x_in[u], x_v[u][:, ds(i * CT, CT), :]).then_inc(s[f"x_in{u}"], 16)
                    sp.wait_ge(s["stage_free"], count(n))
                    sp.dma_start(stage.rearrange("p (k o) -> p k o", k=KB),
                                 ew_v[:, ds(n, 1), :, :].rearrange("p e k o -> p (e k) o")).then_inc(s["stage_in"], 16)
                    sp.wait_ge(s["xl_done"], count((n + 1) * KB))
                    sp.dma_start(xt_v[u][:, ds(i * CT, CT), :],
                                 xhl.rearrange("p t k z c -> p t (k z c)")).then_inc(s["stored"], 16)
                    sp.wait_ge(s["ql_done"], count((n + 1) * KB))
                    for z, a in enumerate((q_hi, q_lo)):
                        sp.dma_start(q_v[z][u][:, :, ds(i * CH, CH)], a).then_inc(s["stored"], 16)
                    sp.wait_ge(s["kl_done"], count((n + 1) * KB))
                    for z, a in enumerate((k_hi, k_lo)):
                        sp.dma_start(k_v[z][u][:, :, ds(i * CH, CH)], a).then_inc(s["stored"], 16)
                    sp.wait_ge(s["v_done"], count((n + 1) * KB))
                    sp.dma_start(v_v[u][:, :, ds(i * (CT * V1), CT * V1)], v_st.rearrange("p h t f -> p h (t f)")).then_inc(s["stored"], 16)
            sp.wait_ge(s["stored"], count(16 * STORES_A * B * NC))

            def load_head(bh, u):
                for st, dram, order in ((q_st[u], q_dram, (0, 0, 1)), (k_st[u], k_dram, (0, 1, 0))):
                    for g, z in enumerate(order):
                        sp.dma_start(st[HD * g:HD * (g + 1), :], dram[z][ds(bh * HD, HD), :]).then_inc(s[f"ld{u}"], 16)
                sp.dma_start(v_sb[u], v_dram[ds(bh, 1), :, :, :].rearrange("o r j f -> (o r) j f")).then_inc(s[f"ld{u}"], 16)

            sp.wait_ge(s["b_zero"], count(1))
            sp.wait_ge(s["stage_free"], count(B * NC))
            load_head(0, 0)
            load_head(1, 1)
            with sp.Fori(0, BH // 2 - 1) as it:
                for u in range(2):
                    sp.wait_ge(s["pv_done"], count(NU * (it * 2 + u + 1)))
                    load_head(it * 2 + u + 2, u)
            sp.wait_ge(s["norm_done"], count(NC * BH))
            with sp.Fori(0, ST) as i:
                for u in range(B):
                    m = i * B + u
                    sp.wait_ge(s["z_ps"], count(since(m * NE, -NE) if u == 0 else (m - 1) * NE))
                    sp.dma_start(xc_t[u].rearrange("p k z c -> p (k z c)"), xt_v[u][:, ds(i, 1), :].rearrange("p g f -> p (g f)")).then_inc(s[f"xt_in{u}"], 16)
                    sp.wait_ge(s["acc_done"], count((i * B)))
                    sp.dma_start(xc[u], xc_v[u][ds(i, 1), :, :].rearrange("t p d -> (t p) d")).then_inc(s[f"xc_in{u}"], 16)
                    if u == 1:
                        for w in range(B):
                            sp.wait_ge(s["acc_done"], count(i * B + w + 1))
                            sp.dma_start(out_v[w][ds(i, 1), :, :].rearrange("t p d -> (t p) d"), acc[w]).then_inc(s[f"out_done{w}"], 16)
            for w in range(B):
                sp.wait_ge(s[f"out_done{w}"], count(16 * ST))

        @block.gpsimd
        def _(pool):
            g = nc.gpsimd
            link, _n = linker(pool, s["pool_link"])
            for t in (bdq, bdk, bdg, bdv, bdo):
                g.memset(t, 0.0)
            g.memset(ws_col[:], WS)
            g.memset(later[:], 0.0)
            g.memset(deny[:], 0.0)
            link(g.memset(eps[:], EPS))
            g.memset(ident[:], 0.0)
            g.memset(ident16[:], 0.0)
            g.memset(center, -1.0 / L)
            g.memset(tri[:], 0.0)
            g.memset(head_of[:], 0.0)
            link(g.memset(of_head[:], 1.0))
            g.sem_inc(s["zeroed"], 1)
            for e in range(NE):
                last = g.memset(iota[:, e:e + 1], float(e))
            link(last)
            for k in range(KB):
                for j in range(HK):
                    link(g.memset(head_of[HD * j:HD * (j + 1), k, k * HK + j:k * HK + j + 1], 1.0 / L))
            for m in (ident, ident16):
                g.affine_select(out=m[:], in_=m[:], compare_op=ALU.not_equal, fill=1.0, base=0,
                                pattern=[[-1, P]], channel_multiplier=1)
            g.affine_select(out=center, in_=center, compare_op=ALU.not_equal, fill=1.0 - 1.0 / L, base=0,
                            pattern=[[-1, P]], channel_multiplier=1)
            g.affine_select(out=tri[:], in_=tri[:], compare_op=ALU.is_ge, fill=LOWEST, base=0,
                            pattern=[[-1, P]], channel_multiplier=1)
            g.affine_select(out=deny[:], in_=deny[:], compare_op=ALU.not_equal, fill=FAR, base=0,
                            pattern=[[-1, P]], channel_multiplier=1)
            g.affine_select(out=later[:], in_=later[:], compare_op=ALU.is_ge, fill=-FAR, base=0,
                            pattern=[[-P, 2], [1, 2 * P]], channel_multiplier=-1)
            link(g.affine_select(out=of_head[:], in_=of_head[:], compare_op=ALU.is_ge, fill=0.0, base=0,
                                 pattern=[[1, KB * P]], channel_multiplier=-HD))
            g.affine_select(out=of_head[:], in_=of_head[:], compare_op=ALU.is_ge, fill=0.0, base=HD - 1,
                            pattern=[[-1, KB * P]], channel_multiplier=HD).then_inc(s["consts"], 1)
            base = _n[0]
            with pool.Fori(0, NC) as i:
                for u in range(B):
                    n = i * B + u
                    lnk, cnt = linker(pool, s["pool_link"], n * 2 + base)
                    pool.wait_ge(s["stage_in"], count((n + 1) * 16))
                    lnk(g.tensor_tensor(stage, stage, ws_col[:].to_broadcast([P, KB * E]), ALU.mult))
                    hi = w_hi[:, ds(n, 1), :].rearrange("p e c -> p (e c)")
                    lo = w_lo[:, ds(n, 1), :].rearrange("p e c -> p (e c)")
                    lnk(g.tensor_copy(hi, stage))
                    g.tensor_tensor(lo, stage, hi, ALU.subtract).then_inc(s["stage_free"], 1)
                    assert cnt[0] == 2
            pool.wait_ge(s["norm_done"], count(NC * BH))
            with pool.Fori(0, ST) as i:
                for u in range(B):
                    m = i * B + u
                    lnk, cnt = linker(pool, s["poolC"], m * (NE + 1))
                    pool.wait_ge(s["otp_ps"], count(since(i * B, 0)))
                    pool.wait_ge(s["r_done"], count(i * B * NE))
                    g.tensor_copy(w_t[:, u, :], route[:, ds(i, 1), u, :].rearrange("p t e -> p (t e)"))
                    g.tensor_copy(o_in[u].rearrange("p (h d) -> p h d", h=H),
                                  attn[:, ds(i, 1), u * H:(u + 1) * H, :].rearrange("p t h d -> p (t h) d")).then_inc(s["o_done"], 1)
                for u in range(B):
                    m = i * B + u
                    lnk, cnt = linker(pool, s["poolC"], m * (NE + 1))
                    pool.wait_ge(s[f"xc_in{u}"], count((i + 1) * 16))
                    pool.wait_ge(s[f"out_done{u}"], count(i * 16))
                    lnk(g.tensor_tensor(acc[u], xc[u], bo_bc[:], ALU.add))
                    for e in range(NE):
                        pool.wait_ge(s["r_done"], count(m * NE + e + 1))
                        lnk(g.tensor_tensor(acc[u], acc[u], r_sb[e % NZ], ALU.add))
                    pool.wait_ge(s["proj_done"], count(m + 1))
                    g.tensor_tensor(acc[u], acc[u], proj[u], ALU.add).then_inc(s["acc_done"], 1)
                    assert cnt[0] == NE + 1

        @block.scalar
        def _(act):
            a = nc.scalar
            with nc.allow_non_contiguous_dma(reason="small per-head vectors, once"):
                act.dma_start(g_t, ln_g.rearrange("h l -> l h")).then_inc(s["g_in"], 16)
                act.dma_start(b_t, ln_b.rearrange("h l -> l h")).then_inc(s["g_in"], 16)
            act.dma_start(gw_raw[:], gate_w.rearrange("(k p) e -> p k e", p=P)).then_inc(s["g_in"], 16)
            act.dma_start(gb_bc[:], gate_b.partition_broadcast(P)).then_inc(s["g_in"], 16)
            act.dma_start(bo_bc[:], bo.partition_broadcast(P)).then_inc(s["g_in"], 16)
            act.dma_start(eb_bc[:], expert_b.partition_broadcast(P)).then_inc(s["g_in"], 16)
            for k in range(KB):
                act.wait_ge(s["wot_ps"], count(k + 1))
                a.activation(wo_t[:, k, :], PS[:, k, :], ACT.Copy).then_inc(s["wot_done"], 1)
            for k in range(KB):
                act.wait_ge(s["comb_ps"], count(k + 1))
                a.activation(comb[:, k, :], PS[:, 4 + k, :], ACT.Copy).then_inc(s["comb_done"], 1)
            with act.Fori(0, NC) as i:
                for u in range(B):
                    n = i * B + u
                    act.wait_ge(s["mv_done"], count(n + 1))
                    a.activation(sd4[:], mv[:, :, 1], ACT.Sqrt, bias=eps[:]).then_inc(s["sd4_done"], 1)
                    act.wait_ge(s["stored"], count(n * 16 * STORES_A))
                    act.wait_ge(s["xr_done"], count(n * KB))
                    for k in range(KB):
                        act.wait_ge(s["tp_ps"], count(n * KB + k + 1))
                        a.activation(x_t[:, k, :], PS[:, k, :], ACT.Copy).then_inc(s["xt_done"], 1)
                    for k in range(KB):
                        act.wait_ge(s["xt_done"], count(n * KB + k + 1))
                        a.activation(xhl[:, :, k, 0, :], x_t[:, k, :].rearrange("p (t c) -> p t c", t=CT),
                                     ACT.Copy).then_inc(s["xh_done"], 1)
                    for k in range(KB):
                        act.wait_ge(s["q_ps"], count(n * KB + k + 1))
                        a.activation(q_hi[:, k, :], PS[:, k, :], ACT.Copy).then_inc(s["qh_done"], 1)
                    act.wait_ge(s["var_ps"], count(n + 1))
                    a.activation(sd_buf[:], PS[0:H, 4, :], ACT.Sqrt, bias=eps[0:H, :]).then_inc(s["sd_done"], 1)
                    for k in range(KB):
                        act.wait_ge(s["k_ps"], count(n * KB + k + 1))
                        a.activation(k_hi[:, k, :], PS[:, k, :], ACT.Identity, bias=bk[:, k:k + 1]).then_inc(s["kh_done"], 1)
            def max_row(sh, w, c):
                act.wait_ge(s["m_ps"], count(sh * NC + c + 1))
                a.activation(q_st[w][3 * HD:3 * HD + 1, c * CH:(c + 1) * CH], PS[3 * HD:3 * HD + 1, 7, :],
                             ACT.Copy).then_inc(s["m_done"], 1)

            def heads(it, more):
                for kk in range(2 * NU + PV_LAG):
                    if kk < 2 * NU:
                        c, j, (wa, wb), off, _m = UNITS[kk % NU]
                        act.wait_ge(s["s2_ps"], count(it * (2 * NU) + kk + 1))
                        act.wait_ge(s["pv_done"], count(since(it * (2 * NU), kk - 3)))
                        z = PS[:, 2 + 2 * (kk % 2):4 + 2 * (kk % 2), :].rearrange("p a s -> p (a s)")
                        a.activation(probs[kk % 4][:, 0:off + wb], z[:, 0:off + wb], ACT.Exp,
                                     scale=SCALE).then_inc(s["exp_done"], 1)
                        u, k = divmod(kk, NU)
                        for ahead, cc in slot_max_rows(k):
                            if u + ahead < 2 or more:
                                max_row(it * 2 + u + ahead, (u + ahead) % 2, cc)
                    pk = kk - PV_LAG
                    if pk >= 0 and pk % NU in LAST:
                        q = (pk // NU) * NC + LAST[pk % NU]
                        act.wait_ge(s["pv_done"], count(it * (2 * NU) + pk + 1))
                        act.wait_ge(s["tr_ps"], count(since(it * (2 * NC), q - 1)))
                        a.activation(ot[q % 2][0:2 * HD + V1, :], PS[0:2 * HD + V1, 6, :], ACT.Copy).then_inc(s["ot_done"], 1)

            for c in range(NC - 1):
                max_row(0, 0, c)
            with act.Fori(0, BH // 2 - 1) as it:
                heads(it, True)
            heads(BH // 2 - 1, False)
            with act.Fori(0, ST) as i:
                for u in range(B):
                    m = i * B + u
                    act.wait_ge(s["otp_ps"], count(m + 1))
                    act.wait_ge(s["proj_ps"], count(since(i * B, 0)))
                    a.activation(o_t[u].rearrange("p k c -> p (k c)"), PS[:, 6 + u, :], ACT.Copy).then_inc(s["otc_done"], 1)
                    for e in range(NE):
                        act.wait_ge(s["z_done"], count(m * NE + e + 1))
                        act.wait_ge(s["poolC"], count(since(i * B * (NE + 1), u * (NE + 1) + e - NZ + 2)))
                        a.activation(r_sb[e % NZ], z_sb[e % NZ], ACT.Relu, scale=w_t[:, u, e:e + 1]).then_inc(s["r_done"], 1)

        @block.vector
        def _(dve):
            v = nc.vector
            link, n0 = linker(dve, s["dve0"])
            dve.wait_ge(s["g_in"], count(96))
            dve.wait_ge(s["w_in"], count(64))

            def per_head(t):
                return t.rearrange("p (h d) -> p h d", h=H)
            for w, r in ((wuk, gwuk), (wuv, gwuv)):
                last = v.tensor_tensor(per_head(r), per_head(w), g_t.unsqueeze(2).to_broadcast([P, H, HD]), ALU.mult)
            last.then_inc(s["gw_done"], 1)
            link(v.tensor_scalar(gw_raw[:], gw_raw[:], WS, None, ALU.mult))
            link(v.tensor_copy(gw_hl[:, 0], gw_raw[:]))
            v.tensor_tensor(gw_hl[:, 1], gw_raw[:], gw_hl[:, 0], ALU.subtract).then_inc(s["gates_done"], 1)
            dve.wait_ge(s["wc_ps"], count(1))
            v.tensor_copy(wc, PS[:, 0, :]).then_inc(s["wc_done"], 1)
            dve.wait_ge(s["fold_ps"], count(1))
            for b, bd in ((1, bdk), (2, bdg), (3, bdv)):
                for j in range(HK):
                    r = slice(HD * j, HD * (j + 1))
                    last = v.tensor_copy(bd[r, :, r], PS[r, b, 0:P].rearrange("p (k c) -> p k c", k=KB))
            v.tensor_copy(bk[:], PS[:, 4, 0:KB])
            v.tensor_copy(bv_bc[:], PS[:, 5, :]).then_inc(s["fold_done"], 1)
            dve.wait_ge(s["consts"], count(1))
            link(v.memset(v_st[:, :, :, HD:V1], 1.0))
            with dve.Fori(0, NC) as i:
                for u in range(B):
                    n = i * B + u
                    lnk, cnt = linker(dve, s["dveA"], n * A_LINKS)
                    dve.wait_ge(s[f"x_in{u}"], count((i + 1) * 16))
                    for t in range(CT):
                        v.bn_stats(stats[:, t, :], x_in[u][:, t, :])
                    v.drain()
                    for t in range(CT):
                        last = v.bn_aggr(mv[:, t, :], stats[:, t, :])
                    last.then_inc(s["mv_done"], 1)
                    dve.wait_ge(s["sd4_done"], count(n + 1))
                    lnk(v.reciprocal(rs4[:], sd4[:]))
                    dve.wait_ge(s["tp_ps"], count(n * KB))
                    for t in range(CT):
                        v.tensor_scalar(xn[:, t, :], x_in[u][:, t, :], mv[:, t, 0:1], rs4[:, t:t + 1],
                                        ALU.subtract, ALU.mult).then_inc(s["xn_done"], 1)
                    for k in range(KB):
                        dve.wait_ge(s["xh_done"], count(n * KB + k + 1))
                        v.tensor_tensor(xhl[:, :, k, 1, :], x_t[:, k, :].rearrange("p (t c) -> p t c", t=CT),
                                        xhl[:, :, k, 0, :], ALU.subtract).then_inc(s["xl_done"], 1)
                    for k in range(KB):
                        dve.wait_ge(s["y_ps"], count(n * KB + k + 1))
                        v.tensor_tensor(prod[:, k, :], PS[:, 4 + k, :], x_t[:, k, :], ALU.mult).then_inc(s["prod_done"], 1)
                    for k in range(KB):
                        dve.wait_ge(s["qh_done"], count(n * KB + k + 1))
                        v.tensor_tensor(q_lo[:, k, :], PS[:, k, :], q_hi[:, k, :], ALU.subtract).then_inc(s["ql_done"], 1)
                    dve.wait_ge(s["lg_ps"], count(n + 1))
                    ins = v.scalar_tensor_tensor(out=lg[:], in0=PS[:, 5, 0:CT * NE].rearrange("p (t e) -> p t e", t=CT),
                                                 scalar=1.0 / WS, in1=gb_bc[:].unsqueeze(1).to_broadcast([P, CT, NE]),
                                                 op0=ALU.mult, op1=ALU.add)
                    ins.then_inc(s["lg_done"], 1)
                    dve.wait_ge(s["sd_done"], count(n + 1))
                    v.reciprocal(rs_row, sd_buf[:]).then_inc(s["rs_done"], 1)
                    v.drain()
                    for t in range(CT):
                        v.max(top8[:, t, :], lg[:, t, :])
                    v.drain()
                    for t in range(CT):
                        v.max_index(idx8[:, t, :], top8[:, t, :], lg[:, t, :])
                    v.drain()
                    lnk(v.tensor_copy(idxf[:], idx8[:]))
                    it8 = iota[:].unsqueeze(1).to_broadcast([P, CT, NE])
                    v.tensor_tensor(eq0[:], it8, idxf[:, :, 0:1].to_broadcast([P, CT, NE]), ALU.is_equal)
                    lnk(v.tensor_tensor(eq1[:], it8, idxf[:, :, 1:2].to_broadcast([P, CT, NE]), ALU.is_equal))
                    lnk(v.tensor_tensor(eq0[:], eq0[:], eq1[:], ALU.add))
                    lnk(v.tensor_scalar(route[:, ds(i * CT, CT), u, :], eq0[:], 0.5, None, ALU.mult))
                    for k in range(KB):
                        dve.wait_ge(s["rb_ps"], count(n * KB + k + 1))
                        v.tensor_tensor(xr[:, k, :], PS[:, 4 + k, :], x_t[:, k, :], ALU.mult).then_inc(s["xr_done"], 1)
                    for k in range(KB):
                        dve.wait_ge(s["kh_done"], count(n * KB + k + 1))
                        v.scalar_tensor_tensor(out=k_lo[:, k, :], in0=PS[:, k, :], scalar=bk[:, k:k + 1],
                                               in1=k_hi[:, k, :], op0=ALU.add, op1=ALU.subtract).then_inc(s["kl_done"], 1)
                    for k in range(KB):
                        dve.wait_ge(s["vv_ps"], count(n * KB + k + 1))
                        v.tensor_tensor(v_st[:, HK * k:HK * (k + 1), :, 0:HD].rearrange("p h t d -> p t h d"),
                                        PS[:, 4 + k, :].rearrange("p (t h d) -> p t h d", t=CT, h=HK),
                                        bv_bc[:, k * P:(k + 1) * P].rearrange("p (h d) -> p h d", h=HK)
                                        .unsqueeze(1).to_broadcast([P, CT, HK, HD]), ALU.add).then_inc(s["v_done"], 1)
                    assert cnt[0] == A_LINKS, cnt
            dve.wait_ge(s["stage_free"], count(B * NC))
            dve.wait_ge(s["stored"], count(16 * STORES_A * B * NC))
            for w in range(2):
                v.memset(k_st[w][3 * HD:3 * HD + 1, :], -MS)
            v.memset(pm[:], LOWEST)
            v.memset(PS[:, 6, :], 0.0).then_inc(s["b_zero"], 1)
            dve.wait_ge(s["b_zero"], count(1))

            def piece(sh, n):
                i, p, w = PIECES[n]
                c, r = divmod(i, CT)
                seq = sh * NP_ + n
                dve.wait_ge(s["s1_ps"], count(seq + 1))
                bank = n % 2
                if p < i // CT:
                    ins = v.reduce_max(pm[:, c, r, p:p + 1], PS[:, bank, 0:w], AX)
                else:
                    v.reduce_max(pm[:, c, r, p:p + 1], PS[:, bank, 0:w - P + 1], AX)
                    ins = v.tensor_tensor_reduce(out=junk[:, r, :], in0=PS[:, bank, w - P:w], in1=tri[:], scale=1.0,
                                                 scalar=LOWEST, op0=ALU.add, op1=ALU.max,
                                                 accum_out=pm[:, c, r, PMS - 1:PMS])
                ins.then_inc(s["s1_done"], 1)
                if n in CHUNK_END:
                    dve.wait_ge(s["s1_done"], count(seq + 1))
                    v.reduce_max(mx[:, c, :], pm[:, c, :, :], AX).then_inc(s["mx_done"], 1)
                    dve.wait_ge(s["mx_done"], count((sh * NC + c) * 2 + 1))
                    v.tensor_scalar(mx16[:, c, :], mx[:, c, :], 1.0 / MS, None, ALU.mult).then_inc(s["mx_done"], 1)

            def norm(it, q):
                lnk, cnt = linker(dve, s["dveB"], (it * (2 * NC) + q) * 3)
                dve.wait_ge(s["tr_ps"], count(it * (2 * NC) + q + 1))
                T = PS[:, 7, 0:CT * (2 * HD + V1)].rearrange("p (t f) -> p t f", t=CT)
                dve.wait_ge(s["norm_done"], count(it * (2 * NC) + q))
                lnk(v.tensor_copy(half_b[:], T[:, :, 2 * HD:2 * HD + V1]))
                lnk(v.tensor_tensor(whole[:], T[:, :, 0:V1], half_b[:], ALU.add))
                lnk(v.reciprocal(rden[:], whole[:, :, HD:V1]))
                u, c = divmod(q, NC)
                v.tensor_tensor(attn[:, CT * c:CT * (c + 1), ds(it * 2 + u, 1), :].rearrange("p t o d -> p t (o d)"),
                                whole[:, :, 0:HD], rden[:].to_broadcast([P, CT, HD]), ALU.mult).then_inc(s["norm_done"], 1)

            def heads(it, more):
                for kk in range(2 * NU + PV_LAG + 1):
                    u, k = divmod(kk, NU)
                    if kk < 2 * NU:
                        for ahead, n in slot_pieces(k):
                            if u + ahead < 2 or more:
                                piece(it * 2 + u + ahead, n)
                    pk = kk - PV_LAG - 1
                    if pk >= 0 and pk % NU in LAST:
                        norm(it, (pk // NU) * NC + LAST[pk % NU])

            for n in range(EARLY):
                piece(0, n)
            with dve.Fori(0, BH // 2 - 1) as it:
                heads(it, True)
            heads(BH // 2 - 1, False)
            with dve.Fori(0, ST) as i:
                for u in range(B):
                    m = i * B + u
                    for e in range(NE):
                        dve.wait_ge(s["z_ps"], count(m * NE + e + 1))
                        dve.wait_ge(s["r_done"], count(since(i * B * NE, u * NE + e - NZ + 1)))
                        v.scalar_tensor_tensor(out=z_sb[e % NZ], in0=PS[:, e % 4, :], scalar=1.0 / WS,
                                               in1=eb_bc[:, e, :], op0=ALU.mult, op1=ALU.add).then_inc(s["z_done"], 1)
                    dve.wait_ge(s["proj_ps"], count(m + 1))
                    dve.wait_ge(s["acc_done"], count(i * B))
                    v.tensor_copy(proj[u], PS[:, 4 + u, :]).then_inc(s["proj_done"], 1)

        @block.tensor
        def _(pe):
            t = nc.tensor
            pe.wait_ge(s["consts"], count(1))
            pe.wait_ge(s["w_in"], count(64))
            t.matmul(PS[:, 0, :], center, wdkv, start=True, stop=True).then_inc(s["wc_ps"], 1)
            pe.wait_ge(s["g_in"], count(96))
            pe.wait_ge(s["wc_done"], count(1))
            pe.wait_ge(s["gw_done"], count(1))
            for h in range(H):
                k, j = divmod(h, HK)
                o = slice(HD * j, HD * (j + 1))
                c = slice(HD * h, HD * (h + 1))
                f = slice(HD * k, HD * (k + 1))
                t.matmul(PS[o, 1, f], wc[:, c], gwuk[:, c], start=True, stop=True)
                t.matmul(PS[o, 2, f], wc[:, c], wc[:, c], start=True, stop=True)
                t.matmul(PS[o, 3, f], wc[:, c], gwuv[:, c], start=True, stop=True)
                t.matmul(PS[o, 4, k:k + 1], wuk[:, c], b_t[:, h:h + 1], start=True, stop=True)
                last = t.matmul(PS[:, 5, c], b_t[:, h:h + 1].to_broadcast([P, P]), wuv[:, c], start=True, stop=True)
            last.then_inc(s["fold_ps"], 1)
            pe.wait_ge(s["fold_done"], count(1))
            for k in range(KB):
                for n in range(4):
                    last = t.transpose(PS[:, k, n * P:(n + 1) * P], wo_raw[:, n, k * P:(k + 1) * P], ident[:])
                last.then_inc(s["wot_ps"], 1)
            pe.wait_ge(s["wqo_in"], count(16 * 2 * HK))
            for k in range(KB):
                pe.wait_ge(s["wot_done"], count(k + 1))
                t.matmul(PS[:, 4 + k, :], bdo[:, k, :], wo_t[:, k, :], start=True, stop=True).then_inc(s["comb_ps"], 1)
            pe.wait_ge(s["comb_done"], count(KB))
            pe.wait_ge(s["gates_done"], count(1))
            with pe.Fori(0, NC) as i:
                for u in range(B):
                    n = i * B + u
                    for tl in range(CT):
                        pe.wait_ge(s["xn_done"], count(n * CT + tl + 1))
                        if tl == 0:
                            pe.wait_ge(s["kl_done"], count(n * KB))
                        for k in range(KB):
                            last = t.transpose(PS[:, k, tl * P:(tl + 1) * P], xn[:, tl, k * P:(k + 1) * P], ident[:])
                            if tl == CT - 1:
                                last.then_inc(s["tp_ps"], 1)
                    pe.wait_ge(s["v_done"], count(n * KB))
                    for k in range(KB):
                        pe.wait_ge(s["xt_done"], count(n * KB + k + 1))
                        t.matmul(PS[:, 4 + k, :], bdg[:, k, :], x_t[:, k, :], start=True, stop=True).then_inc(s["y_ps"], 1)
                        t.matmul(PS[:, k, :], bdq[:, k, :], x_t[:, k, :], start=True, stop=True).then_inc(s["q_ps"], 1)
                    pe.wait_ge(s["prod_done"], count(n * KB + KB))
                    pe.wait_ge(s["xl_done"], count(n * KB + KB))
                    for tl in range(CT):
                        terms = [(k, z, y) for k in range(KB) for z in range(2) for y in range(2)]
                        for q, (k, z, y) in enumerate(terms):
                            last = t.matmul(PS[:, 5, tl * NE:(tl + 1) * NE], xhl[:, tl, k, z, :], gw_hl[:, y, k, :],
                                            start=q == 0, stop=q == len(terms) - 1)
                    last.then_inc(s["lg_ps"], 1)
                    for k in range(KB):
                        last = t.matmul(PS[0:H, 4, :], head_of[:, k, :], prod[:, k, :], start=k == 0, stop=k == KB - 1)
                    last.then_inc(s["var_ps"], 1)
                    pe.wait_ge(s["rs_done"], count(n + 1))
                    pe.wait_ge(s["lg_done"], count(n + 1))
                    for k in range(KB):
                        t.matmul(PS[:, 4 + k, :], of_head[:, k * P:(k + 1) * P], rs_row, start=True,
                                 stop=True).then_inc(s["rb_ps"], 1)
                    for k in range(KB):
                        pe.wait_ge(s["xr_done"], count(n * KB + k + 1))
                        pe.wait_ge(s["ql_done"], count(n * KB + k + 1))
                        t.matmul(PS[:, k, :], bdk[:, k, :], xr[:, k, :], start=True, stop=True).then_inc(s["k_ps"], 1)
                        for tl in range(CT):
                            last = t.matmul(PS[:, 4 + k, tl * P:(tl + 1) * P], xr[:, k, tl * P:(tl + 1) * P],
                                            bdv[:, k, :], start=True, stop=True)
                        last.then_inc(s["vv_ps"], 1)
            pe.wait_ge(s["kl_done"], count(B * NC * KB))
            pe.wait_ge(s["v_done"], count(B * NC * KB))
            pe.wait_ge(s["b_zero"], count(1))

            def piece(sh, w, n, first):
                i, p, wd = PIECES[n]
                if not (first and n < 2):
                    pe.wait_ge(s["s1_done"], count(sh * NP_ + n - 1))
                t.matmul(PS[:, n % 2, 0:wd], q_st[w][0:3 * HD, i * P:(i + 1) * P], k_st[w][0:3 * HD, p * CH:p * CH + wd],
                         start=True, stop=True).then_inc(s["s1_ps"], 1)

            def max_row(sh, w, c, normed):
                pe.wait_ge(s["mx_done"], count((sh * NC + c + 1) * 2))
                pe.wait_ge(s["norm_done"], count(normed))
                pe.wait_ge(s["m_done"], count(sh * NC + c))
                for r in range(CT):
                    last = t.matmul(PS[3 * HD:3 * HD + 1, 7, r * P:(r + 1) * P], mx16[:, c, r:r + 1], ident16[:],
                                    start=True, stop=True)
                last.then_inc(s["m_ps"], 1)

            def heads(it, more):
                made = 0
                rows = 0
                for kk in range(2 * NU + PV_LAG + 1):
                    u, k = divmod(kk, NU)
                    if kk < 2 * NU:
                        c, j, wds, off, diag = UNITS[k]
                        pe.wait_ge(s["exp_done"], count(since(it * (2 * NU), kk - 1)))
                        if k in FIRST:
                            pe.wait_ge(s["m_done"], count((it * 2 + u) * NC + c + 1))
                        z = PS[:, 2 + 2 * (kk % 2):4 + 2 * (kk % 2), :].rearrange("p a s -> p (a s)")
                        beside = [(ahead, n) for ahead, n in slot_pieces(k) if u + ahead < 2 or more]
                        if k == S1_FROM and beside:
                            pe.wait_ge(s[f"ld{1 - u}"], count((it + 1 + u) * LOADS))
                        for a in range(2):
                            at = a * off
                            last = t.matmul(z[:, at:at + wds[a]], k_st[u][0:3 * HD + 1, (j + a) * P:(j + a + 1) * P],
                                            q_st[u][0:3 * HD + 1, (c + 1) * CH - wds[a]:(c + 1) * CH],
                                            start=True, stop=not diag)
                            if diag:
                                wm = 2 * P if (c, j, a) == (0, 0, 1) else P
                                last = t.matmul(z[:, at:at + wm], deny[:], later[:, int(wm > P), 0:wm], start=False, stop=True)
                            if a == 0 and beside:
                                ahead, n = beside[0]
                                piece(it * 2 + u + ahead, (u + ahead) % 2, n, False)
                        last.then_inc(s["s2_ps"], 1)
                    else:
                        beside = []
                    pk = kk - PV_LAG
                    piece_first = 0 <= pk < 2 * NU and pk % NU in FIRST
                    if beside and piece_first:
                        ahead, n = beside[1]
                        piece(it * 2 + u + ahead, (u + ahead) % 2, n, False)
                    if 0 <= pk < 2 * NU:
                        pu, p_ = divmod(pk, NU)
                        c, j, wds, off, _m = UNITS[p_]
                        pe.wait_ge(s["exp_done"], count(it * (2 * NU) + pk + 1))
                        if p_ in FIRST:
                            pe.wait_ge(s["ot_done"], count(it * (2 * NC) + pu * NC + c))
                        for a in range(2):
                            rows_ = slice(2 * HD * a, 2 * HD * a + V1)
                            last = t.matmul(PS[rows_, 6, CH - wds[a]:CH], v_sb[pu][:, j + a, :],
                                            probs[pk % 4][:, a * off:a * off + wds[a]],
                                            start=p_ in FIRST, stop=p_ in LAST)
                        last.then_inc(s["pv_done"], 1)
                    if beside and not piece_first:
                        ahead, n = beside[1]
                        piece(it * 2 + u + ahead, (u + ahead) % 2, n, False)
                    if kk < 2 * NU:
                        for ahead, cc in slot_max_rows(k):
                            if u + ahead < 2 or more:
                                max_row(it * 2 + u + ahead, (u + ahead) % 2, cc, it * (2 * NC) + made)
                                rows += 1
                    tk = kk - PV_LAG - 1
                    if tk >= 0 and tk % NU in LAST:
                        q = (tk // NU) * NC + LAST[tk % NU]
                        pe.wait_ge(s["ot_done"], count(it * (2 * NC) + q + 1))
                        pe.wait_ge(s["norm_done"], count(it * (2 * NC) + q))
                        pe.wait_ge(s["m_done"], count(it * (2 * NC) + NC - 1 + rows))
                        for r in range(CT):
                            W_ = 2 * HD + V1
                            last = t.transpose(PS[:, 7, r * W_:(r + 1) * W_], ot[q % 2][0:W_, r * P:(r + 1) * P], ident[0:W_, 0:W_])
                        last.then_inc(s["tr_ps"], 1)
                        made += 1

            LOADS = 7 * 16
            pe.wait_ge(s["ld0"], count(LOADS))
            for n in range(EARLY):
                piece(0, 0, n, True)
                if n in CHUNK_END:
                    max_row(0, 0, CHUNK_END[n], 0)
            with pe.Fori(0, BH // 2 - 1) as it:
                heads(it, True)
            heads(BH // 2 - 1, False)
            pe.wait_ge(s["norm_done"], count(NC * BH))
            with pe.Fori(0, ST) as i:
                for u in range(B):
                    m = i * B + u
                    pe.wait_ge(s["o_done"], count(m + 1))
                    pe.wait_ge(s["otc_done"], count(i * B))
                    for k in range(KB):
                        last = t.transpose(PS[:, 6 + u, k * P:(k + 1) * P], o_in[u][:, k * P:(k + 1) * P], ident[:])
                    last.then_inc(s["otp_ps"], 1)
                    pe.wait_ge(s[f"xt_in{u}"], count((i + 1) * 16))
                    for e in range(NE):
                        pe.wait_ge(s["z_done"], count(since(i * B * NE, u * NE + e - 3)))
                        terms = [(k, z, w) for k in range(KB) for z, w in ((0, w_hi), (1, w_hi), (0, w_lo))]
                        for q, (k, z, w) in enumerate(terms):
                            last = t.matmul(PS[:, e % 4, :], xc_t[u][:, k, z, :], w[:, e, k * E:(k + 1) * E],
                                            start=q == 0, stop=q == len(terms) - 1)
                        last.then_inc(s["z_ps"], 1)
                        if e == 3:
                            pe.wait_ge(s["otc_done"], count(m + 1))
                            pe.wait_ge(s["proj_done"], count(i * B))
                            for k in range(KB):
                                last = t.matmul(PS[:, 4 + u, :], o_t[u][:, k, :], comb[:, k, :], start=k == 0, stop=k == KB - 1)
                            last.then_inc(s["proj_ps"], 1)


_INS = ["x", "Wq", "Wdkv", "Wuk", "Wuv", "ln_g", "ln_b", "Wo_h", "Wo", "bo", "gate_w", "gate_b", "expert_w", "expert_b"]


def kernel(L0_attn_x, L0_attn_Wq, L0_attn_Wdkv, L0_attn_Wuk, L0_attn_Wuv, L0_attn_ln_g, L0_attn_ln_b, L0_attn_Wo_h,
           L0_attn_Wo, L0_attn_bo, L0_ffn_gate_w, L0_ffn_gate_b, L0_ffn_expert_w, L0_ffn_expert_b):
    import numpy as _np
    import concourse.bacc as _bacc
    from concourse import mybir as _mybir
    from concourse.bass_utils import run_bass_kernel_spmd as _run

    given = [L0_attn_x, L0_attn_Wq, L0_attn_Wdkv, L0_attn_Wuk, L0_attn_Wuv, L0_attn_ln_g, L0_attn_ln_b, L0_attn_Wo_h,
             L0_attn_Wo, L0_attn_bo, L0_ffn_gate_w, L0_ffn_gate_b, L0_ffn_expert_w, L0_ffn_expert_b]
    nc = _bacc.Bacc("TRN2", target_bir_lowering=False, num_devices=1)
    arrays, args = {}, []
    for name, value in zip(_INS, given):
        a = _np.ascontiguousarray(value)
        arrays[f"in_{name}"] = a
        args.append(nc.dram_tensor(f"in_{name}", a.shape, _mybir.dt.from_np(a.dtype), kind="ExternalInput").ap())
    out = nc.dram_tensor("out_0", tuple(L0_attn_x.shape), _mybir.dt.float32, kind="ExternalOutput").ap()
    layer_kernel(nc, *args, out)
    r = _run(nc, [arrays], core_ids=[0])
    return r.results[0]["out_0"]
```

```python
import concourse.bass as bass
from concourse import mybir
from contextlib import ExitStack


def layer_kernel(nc, x, Wq, Wdkv, Wuk, Wuv, ln_g, ln_b, Wo_h, Wo, bo,
                 gate_w, gate_b, expert_w, expert_b, out):
    f32, f16, u32, i32 = mybir.dt.float32, mybir.dt.float16, mybir.dt.uint32, mybir.dt.int32
    ALU, ACT, AX = mybir.AluOpType, mybir.ActivationFunctionType, mybir.AxisListType.X
    ds = bass.ds

    B, S, E = x.shape
    H, L, HD = Wdkv.shape
    NE = gate_w.shape[1]
    P = 128
    KB = E // P
    HK = P // HD
    CH = 512
    CT = CH // P
    NC = S // CH
    ST = S // P
    BH = B * H
    V1 = HD + 1
    SCALE = 1.0 / float(L) ** 0.5
    WS = 256.0
    TOP = 2
    NT = B * ST
    PT = -(-(NT * TOP + NE - 1) // 2) * 2
    MS = 64.0
    LOWEST = -3.0e38
    FAR = 32768.0
    EPS = 1e-5

    q_dram = nc.dram_tensor("q_pieces", (2, BH * HD, S), f16, kind="Internal").ap()
    k_dram = nc.dram_tensor("k_pieces", (2, BH * HD, S), f16, kind="Internal").ap()
    v_dram = nc.dram_tensor("v_rows", (BH, P, ST, V1), f32, kind="Internal").ap()
    xn_dram = nc.dram_tensor("xn_rows", (NT * P, E), f32, kind="Internal").ap()
    id_dram = nc.dram_tensor("token_of_place", (P * PT, 1), u32, kind="Internal").ap()
    y_dram = nc.dram_tensor("expert_rows", (PT * P, E), f32, kind="Internal").ap()

    ctx = ExitStack()
    with ctx:
        def sb(name, shape, dt):
            return ctx.enter_context(nc.sbuf_tensor(name, shape, dt))

        def sem(name):
            return ctx.enter_context(nc.semaphore(name))

        arena1 = sb("arena1", [P, 16384], f32)
        arena2 = sb("arena2", [P, 10304], f32)
        w_hi = sb("w_hi", [P, NE, KB * E], f16)
        w_lo = sb("w_lo", [P, NE, KB * E], f16)
        eb_bc = sb("eb_bc", [P, NE, E], f32)
        comb = sb("comb", [P, KB, E], f32)
        bo_bc = sb("bo_bc", [P, E], f32)
        bv_bc = sb("bv_bc", [P, E], f32)
        ident = sb("ident", [P, P], f32)
        ident16 = sb("ident16", [P, P], f16)
        tri = sb("tri", [P, P], f32)
        head_of = sb("head_of", [P, KB, H], f32)
        of_head = sb("of_head", [H, KB * P], f32)
        bk = sb("bk", [P, KB], f32)
        gw_hl = sb("gw_hl", [P, 2, KB, NE], f16)
        gw_raw = sb("gw_raw", [P, KB, NE], f32)
        gb_bc = sb("gb_bc", [P, NE], f32)
        eps = sb("eps", [P, 1], f32)
        ws_col = sb("ws_col", [P, 1], f32)
        deny = sb("deny", [P, P], f16)
        later = sb("later", [P, 2, 2 * P], f16)
        iota = sb("iota", [P, PT], f32)
        chosen = sb("chosen", [P, TOP, NT, NE], f16)
        place = sb("place", [P, TOP, NT], u32)
        place_at = sb("place_at", [P, TOP, NT], u32)
        expert_of = sb("expert_of", [P, PT], i32)
        upper = sb("upper", [P, P], f16)
        zero_ids = sb("zero_ids", [P, PT], u32)
        token_id = sb("token_id", [P, NT], u32)
        cur = sb("cur", [P, 2 * TOP], u32)
        cur_id = sb("cur_id", [P, 2], u32)

        def carve(arena):
            at = [0]

            def take(n, dt=f32):
                w = n if dt == f32 else n // 2
                a = arena[:, at[0]:at[0] + w]
                at[0] += w
                assert at[0] <= arena.shape[1], at[0]
                return a if dt == f32 else a.bitcast(dt)
            return take

        t0 = carve(arena1)
        wdkv = t0(H * HD)
        wuk = t0(H * HD)
        wuv = t0(H * HD)
        wc = t0(H * HD)
        gwuk = t0(H * HD)
        gwuv = t0(H * HD)
        g_t = t0(H)
        b_t = t0(H)
        center = t0(P)
        bdo = t0(KB * P).rearrange("p (k c) -> p k c", k=KB)
        wo_raw = t0(4 * E).rearrange("p (n c) -> p n c", n=4)
        wo_t = t0(KB * E).rearrange("p (k c) -> p k c", k=KB)
        tA = carve(arena2)
        xhl = tA(CT * KB * 2 * P, f16).rearrange("p (t k z c) -> p t k z c", t=CT, k=KB, z=2)
        q_hi, q_lo, k_hi, k_lo = (tA(KB * CH, f16).rearrange("p (k s) -> p k s", k=KB) for _ in range(4))
        v_st = tA(CT * H * V1).rearrange("p (h t f) -> p h t f", t=CT, h=H)
        stage = tA(KB * E)
        tA = carve(arena1)
        tA(6 * CT * E)
        bdq, bdk, bdg, bdv = (tA(KB * P).rearrange("p (k c) -> p k c", k=KB) for _ in range(4))
        small = tA(CH)
        sd_buf = tA(CH)[0:H, :]
        tA = carve(arena1)
        x_in = [tA(CT * E).rearrange("p (t c) -> p t c", t=CT) for _ in range(2)]
        xn = tA(CT * E).rearrange("p (t c) -> p t c", t=CT)
        x_t = tA(KB * CH).rearrange("p (k s) -> p k s", k=KB)
        prod = tA(KB * CH).rearrange("p (k s) -> p k s", k=KB)
        xr = tA(KB * CH).rearrange("p (k s) -> p k s", k=KB)
        rs_row = small[0:H, 0:CH]
        stats = sb("stats", [P, CT, 6], f32)
        mv = sb("mv", [P, CT, 2], f32)
        sd4 = sb("sd4", [P, CT], f32)
        rs4 = sb("rs4", [P, CT], f32)
        lg = sb("lg", [P, CT, NE], f32)
        top8 = sb("top8", [P, CT, 8], f32)
        idx8 = sb("idx8", [P, CT, 8], u32)
        idxf = sb("idxf", [P, CT, 8], f32)
        attn = arena1[:, :].rearrange("p (t g d) -> p t g d", t=ST, g=BH)
        tB = carve(arena2)
        probs = [tB(2 * CH) for _ in range(4)]
        q_st = [tB(S, f16) for _ in range(2)]
        k_st = [tB(S, f16) for _ in range(2)]
        v_sb = [tB(ST * V1).rearrange("p (j f) -> p j f", j=ST) for _ in range(2)]
        ot = [tB(CH) for _ in range(2)]
        PMS = 6
        pm = sb("pm", [P, NC, CT, PMS], f32)
        mx = sb("mx", [P, NC, CT], f32)
        mx16 = sb("mx16", [P, NC, CT], f16)
        half_b = sb("half_b", [P, CT, V1], f32)
        whole = sb("whole", [P, CT, V1], f32)
        rden = sb("rden", [P, CT, 1], f32)
        tR = carve(arena1)
        r_m16 = tR(NT * NE, f16)
        r_in, r_tot, r_incl, r_slot, r_tmp = (tR(NT * NE) for _ in range(5))
        r_n, r_tiles, r_cum, r_base = (tR(NE) for _ in range(4))
        r_int = tR(NT * TOP).bitcast(i32)
        r_int2 = tR(NT * TOP).bitcast(i32)
        r_f = tR(NT * TOP)
        r_exp = tR(PT)
        r_ones = tR(NT)
        ones16 = tR(P, f16)
        tD = carve(arena2)
        x_g = [tD(E) for _ in range(2)]
        xg_hi = [tD(E, f16).rearrange("p (k c) -> p k c", k=KB) for _ in range(2)]
        xg_lo = [tD(E, f16).rearrange("p (k c) -> p k c", k=KB) for _ in range(2)]
        z_sb = [tD(E) for _ in range(2)]
        y_sb = [tD(E) for _ in range(2)]
        ids = tD(PT).bitcast(u32)
        tC = carve(arena2)
        tC(8 * E)
        xc = [tC(E) for _ in range(B)]
        o_in = [tC(E) for _ in range(B)]
        o_t = [tC(E).rearrange("p (k c) -> p k c", k=KB) for _ in range(B)]
        acc = [tC(E) for _ in range(B)]
        y_g = [[tC(E) for _ in range(TOP)] for _ in range(B)]
        junk = bv_bc[:, :].rearrange("p (r c) -> p r c", r=CT)

        PS = ctx.enter_context(nc.psum_tensor("PS", [P, 8, CH], f32))

        s = {n: sem(n) for n in (
            "w_in wqo_in g_in zeroed consts wc_ps wc_done gw_done fold_ps fold_done bk_ps bk_done bv_ps bv_done "
            "wot_ps wot_done comb_ps comb_done gates_done dve0 "
            "x_in0 x_in1 stage_in stage_free pool_link sd4_done xn_done tp_ps xt_done xh_done xl_done y_ps prod_done "
            "var_ps sd_done rs_done rb_ps xr_done q_ps qh_done ql_done k_ps kh_done kl_done vv_ps v_done lg_ps lg_done "
            "stored xn_st dveA mv_done "
            "ld0 ld1 b_zero s1_ps s1_done mx_done m_ps m_done s2_ps exp_done pv_done ot_done tr_ps norm_done dveB "
            "counted cnt_ps cnt_done placed dveR id_zero id_done ids_in cur_done xg_in0 xg_in1 gt_ps gh_done gl_done "
            "z_ps z_done y_done y_st0 y_st1 "
            "xc_in0 xc_in1 o_done otp_ps otc_done proj_ps cure_done yg_in0 yg_in1 acc_done out_done0 out_done1 dveE"
        ).split()}

        def linker(engine, semaphore, base=0):
            n = [0]

            def link(ins):
                n[0] += 1
                ins.then_inc(semaphore, 1)
                engine.wait_ge(semaphore, count(base + n[0]))
            return link, n

        START = 4
        FROM_ZERO = ("id_zero", "id_done", "ids_in", "xg_in0", "xg_in1", "yg_in0", "yg_in1")

        def count(n):
            return n + START

        def start(engine, part):
            for semaphore in [s[name] for name in s if name not in FROM_ZERO][part::5]:
                engine.sem_inc(semaphore, START)

        block = ctx.enter_context(nc.Block())

        x_v = x.rearrange("b (g p) d -> b p g d", p=P)
        q_v = q_dram.rearrange("z (b k r) s -> z b r k s", b=B, k=KB)
        k_v = k_dram.rearrange("z (b k r) s -> z b r k s", b=B, k=KB)
        v_v = v_dram.rearrange("(b h) r j f -> b r h (j f)", b=B)
        xn_v = xn_dram.rearrange("(b g p) d -> b p g d", b=B, p=P)
        ew_v = expert_w.rearrange("e (k p) o -> p e k o", p=P)
        out_v = out.rearrange("b (t p) d -> b t p d", p=P)
        xc_v = x.rearrange("b (t p) d -> b t p d", p=P)

        STORES_A = 5
        A_LINKS = 2

        def head_units():
            units = []
            for c in range(NC):
                d0 = CT * c
                if c == 0:
                    own = [(c, 0, (CH, CH), CH, True), (c, 2, (2 * P, P), 2 * P, True)]
                    units += own
                    continue
                full = [(c, j, (CH, CH), CH, False) for j in range(0, d0, 2)]
                diag = [(c, d0, (CH, CH - P), CH, True), (c, d0 + 2, (2 * P, P), 2 * P, True)]
                units += full[:1] + diag + full[1:]
            return units

        UNITS = head_units()
        NU = len(UNITS)
        LAST = {max(k for k, un in enumerate(UNITS) if un[0] == c): c for c in range(NC)}
        FIRST = {min(k for k, un in enumerate(UNITS) if un[0] == c): c for c in range(NC)}
        PIECES = [(i, p, min(CH, P * (i + 1) - CH * p)) for i in range(ST) for p in range(i // CT + 1)]
        NP_ = len(PIECES)
        PV_LAG = 2
        S1_FROM = 5
        EARLY = NP_ - 2 * S1_FROM

        def slot_pieces(k):
            if k < S1_FROM:
                return [(0, EARLY + 2 * k), (0, EARLY + 2 * k + 1)]
            return [(1, 2 * (k - S1_FROM)), (1, 2 * (k - S1_FROM) + 1)]

        CHUNK_END = {max(n for n, pc in enumerate(PIECES) if pc[0] // CT == c): c for c in range(NC)}

        def slot_max_rows(k):
            done = slot_pieces(k - 1) if k else []
            return [(ahead, CHUNK_END[n]) for ahead, n in done if n in CHUNK_END]

        assert 2 * (NU - S1_FROM) == EARLY and (NP_ - 1) // 2 * 2 + 1 == NP_ - 1

        @block.sync
        def _(sp):
            start(sp, 0)
            sp.dma_start(wdkv.rearrange("p (h d) -> p h d", h=H), Wdkv.rearrange("h l d -> l h d")).then_inc(s["w_in"], 16)
            sp.dma_start(wuk.rearrange("p (h d) -> p h d", h=H), Wuk.rearrange("h l d -> l h d")).then_inc(s["w_in"], 16)
            sp.dma_start(wuv.rearrange("p (h d) -> p h d", h=H), Wuv.rearrange("h l d -> l h d")).then_inc(s["w_in"], 16)
            sp.dma_start(wo_raw, Wo.rearrange("(n p) c -> p n c", p=P)).then_inc(s["w_in"], 16)
            sp.wait_ge(s["zeroed"], count(1))
            for j in range(HK):
                r = slice(HD * j, HD * (j + 1))
                sp.dma_start(bdq[r, :, r], Wq.rearrange("(k j) i o -> j i k o", j=HK)[j]).then_inc(s["wqo_in"], 16)
                sp.dma_start(bdo[r, :, r], Wo_h.rearrange("(k j) e d -> j e k d", j=HK)[j]).then_inc(s["wqo_in"], 16)
            sp.wait_ge(s["comb_done"], count(KB))
            with sp.Fori(0, NC) as i:
                for u in range(B):
                    n = i * B + u
                    sp.wait_ge(s["xn_done"], count(n * CT))
                    sp.dma_start(x_in[u], x_v[u][:, ds(i * CT, CT), :]).then_inc(s[f"x_in{u}"], 16)
                    sp.wait_ge(s["stage_free"], count(n))
                    sp.dma_start(stage.rearrange("p (k o) -> p k o", k=KB),
                                 ew_v[:, ds(n, 1), :, :].rearrange("p e k o -> p (e k) o")).then_inc(s["stage_in"], 16)
                    sp.wait_ge(s["xn_done"], count((n + 1) * CT))
                    sp.dma_start(xn_v[u][:, ds(i * CT, CT), :], xn).then_inc(s["xn_st"], 16)
                    sp.wait_ge(s["ql_done"], count((n + 1) * KB))
                    for z, a in enumerate((q_hi, q_lo)):
                        sp.dma_start(q_v[z][u][:, :, ds(i * CH, CH)], a).then_inc(s["stored"], 16)
                    sp.wait_ge(s["kl_done"], count((n + 1) * KB))
                    for z, a in enumerate((k_hi, k_lo)):
                        sp.dma_start(k_v[z][u][:, :, ds(i * CH, CH)], a).then_inc(s["stored"], 16)
                    sp.wait_ge(s["v_done"], count((n + 1) * KB))
                    sp.dma_start(v_v[u][:, :, ds(i * (CT * V1), CT * V1)], v_st.rearrange("p h t f -> p h (t f)")).then_inc(s["stored"], 16)
            sp.wait_ge(s["stored"], count(16 * STORES_A * B * NC))

            def load_head(bh, u):
                for st, dram, order in ((q_st[u], q_dram, (0, 0, 1)), (k_st[u], k_dram, (0, 1, 0))):
                    for g, z in enumerate(order):
                        sp.dma_start(st[HD * g:HD * (g + 1), :], dram[z][ds(bh * HD, HD), :]).then_inc(s[f"ld{u}"], 16)
                sp.dma_start(v_sb[u], v_dram[ds(bh, 1), :, :, :].rearrange("o r j f -> (o r) j f")).then_inc(s[f"ld{u}"], 16)

            sp.wait_ge(s["b_zero"], count(1))
            sp.wait_ge(s["stage_free"], count(B * NC))
            load_head(0, 0)
            load_head(1, 1)
            with sp.Fori(0, BH // 2 - 1) as it:
                for u in range(2):
                    sp.wait_ge(s["pv_done"], count(NU * (it * 2 + u + 1)))
                    load_head(it * 2 + u + 2, u)
            with sp.Fori(0, PT // 2) as i:
                for u in range(2):
                    sp.wait_ge(s["y_done"], count(i * 2 + u + 1))
                    sp.dma_start(y_dram[ds((i * 2 + u) * P, P), :], y_sb[u]).then_inc(s[f"y_st{u}"], 16)
            with sp.Fori(0, ST) as i:
                for u in range(B):
                    sp.wait_ge(s["acc_done"], count(i * B))
                    sp.dma_start(xc[u], xc_v[u][ds(i, 1), :, :].rearrange("t p d -> (t p) d")).then_inc(s[f"xc_in{u}"], 16)
                for u in range(B):
                    sp.wait_ge(s["acc_done"], count(i * B + u + 1))
                    sp.dma_start(out_v[u][ds(i, 1), :, :].rearrange("t p d -> (t p) d"), acc[u]).then_inc(s[f"out_done{u}"], 16)
            for w in range(B):
                sp.wait_ge(s[f"out_done{w}"], count(16 * ST))

        @block.gpsimd
        def _(pool):
            g = nc.gpsimd
            start(pool, 1)
            link, _n = linker(pool, s["pool_link"])
            for t in (bdq, bdk, bdg, bdv, bdo):
                g.memset(t, 0.0)
            g.memset(ws_col[:], WS)
            g.memset(later[:], 0.0)
            g.memset(deny[:], 0.0)
            link(g.memset(eps[:], EPS))
            g.memset(ident[:], 0.0)
            g.memset(ident16[:], 0.0)
            g.memset(center, -1.0 / L)
            g.memset(tri[:], 0.0)
            g.memset(head_of[:], 0.0)
            link(g.memset(of_head[:], 1.0))
            g.sem_inc(s["zeroed"], 1)
            g.iota(iota[:], [[1, PT]], base=0, channel_multiplier=0, allow_small_or_imprecise_dtypes=True)
            g.memset(upper[:], 1.0)
            g.iota(token_id[:], [[P, NT]], base=0, channel_multiplier=1)
            link(g.memset(zero_ids[:], 0))
            g.affine_select(out=upper[:], in_=upper[:], compare_op=ALU.is_gt, fill=0.0, base=0,
                            pattern=[[1, P]], channel_multiplier=-1)
            for k in range(KB):
                for j in range(HK):
                    link(g.memset(head_of[HD * j:HD * (j + 1), k, k * HK + j:k * HK + j + 1], 1.0 / L))
            for m in (ident, ident16):
                g.affine_select(out=m[:], in_=m[:], compare_op=ALU.not_equal, fill=1.0, base=0,
                                pattern=[[-1, P]], channel_multiplier=1)
            g.affine_select(out=center, in_=center, compare_op=ALU.not_equal, fill=1.0 - 1.0 / L, base=0,
                            pattern=[[-1, P]], channel_multiplier=1)
            g.affine_select(out=tri[:], in_=tri[:], compare_op=ALU.is_ge, fill=LOWEST, base=0,
                            pattern=[[-1, P]], channel_multiplier=1)
            g.affine_select(out=deny[:], in_=deny[:], compare_op=ALU.not_equal, fill=FAR, base=0,
                            pattern=[[-1, P]], channel_multiplier=1)
            g.affine_select(out=later[:], in_=later[:], compare_op=ALU.is_ge, fill=-FAR, base=0,
                            pattern=[[-P, 2], [1, 2 * P]], channel_multiplier=-1)
            link(g.affine_select(out=of_head[:], in_=of_head[:], compare_op=ALU.is_ge, fill=0.0, base=0,
                                 pattern=[[1, KB * P]], channel_multiplier=-HD))
            g.affine_select(out=of_head[:], in_=of_head[:], compare_op=ALU.is_ge, fill=0.0, base=HD - 1,
                            pattern=[[-1, KB * P]], channel_multiplier=HD).then_inc(s["consts"], 1)
            base = _n[0]
            with pool.Fori(0, NC) as i:
                for u in range(B):
                    n = i * B + u
                    lnk, cnt = linker(pool, s["pool_link"], n * 2 + base)
                    pool.wait_ge(s["stage_in"], count((n + 1) * 16))
                    lnk(g.tensor_tensor(stage, stage, ws_col[:].to_broadcast([P, KB * E]), ALU.mult))
                    hi = w_hi[:, ds(n, 1), :].rearrange("p e c -> p (e c)")
                    lo = w_lo[:, ds(n, 1), :].rearrange("p e c -> p (e c)")
                    lnk(g.tensor_copy(hi, stage))
                    g.tensor_tensor(lo, stage, hi, ALU.subtract).then_inc(s["stage_free"], 1)
                    assert cnt[0] == 2
            pool.dma_start(id_dram.rearrange("(p t) o -> p (t o)", p=P), zero_ids[:]).then_inc(s["id_zero"], 16)
            pool.wait_ge(s["id_zero"], 16)
            pool.wait_ge(s["placed"], count(1))
            with pool.Fori(0, NT) as i:
                g.tensor_copy(cur[:, 0:TOP], place_at[:, :, ds(i, 1)].rearrange("p k o -> p (k o)"))
                g.tensor_copy(cur_id[:, 0:1], token_id[:, ds(i, 1)])
                g.drain()
                for k in range(TOP):
                    g.indirect_dma_start(out=id_dram, out_offset=bass.IndirectOffsetOnAxis(ap=cur[:, k:k + 1], axis=0),
                                         in_=cur_id[:, 0:1], in_offset=None).then_inc(s["id_done"], 16)
                pool.wait_ge(s["id_done"], (i + 1) * (16 * TOP))
            pool.wait_ge(s["id_done"], 16 * TOP * NT)
            pool.wait_ge(s["norm_done"], count(NC * BH))
            pool.dma_start(ids, id_dram.rearrange("(p t) o -> p (t o)", p=P)).then_inc(s["ids_in"], 16)
            pool.wait_ge(s["ids_in"], 16)
            with pool.Fori(0, PT // 2) as i:
                for u in range(2):
                    pool.wait_ge(s["gt_ps"], count(i * 2 + u - 1))
                    g.tensor_copy(cur_id[:, u:u + 1], ids[:, ds(i * 2 + u, 1)])
                    g.drain()
                    g.indirect_dma_start(out=x_g[u], out_offset=None, in_=xn_dram,
                                         in_offset=bass.IndirectOffsetOnAxis(ap=cur_id[:, u:u + 1], axis=0)
                                         ).then_inc(s[f"xg_in{u}"], 16)
            for u in range(2):
                pool.wait_ge(s[f"y_st{u}"], count(16 * PT // 2))
            with pool.Fori(0, ST) as i:
                for u in range(B):
                    pool.wait_ge(s["acc_done"], count(i * B + u - 1))
                    g.tensor_copy(cur[:, TOP * u:TOP * (u + 1)], place[:, :, ds(i + u * ST, 1)].rearrange("p k o -> p (k o)"))
                    g.drain()
                    for k in range(TOP):
                        g.indirect_dma_start(out=y_g[u][k], out_offset=None, in_=y_dram,
                                             in_offset=bass.IndirectOffsetOnAxis(ap=cur[:, TOP * u + k:TOP * u + k + 1], axis=0)
                                             ).then_inc(s[f"yg_in{u}"], 16)

        @block.scalar
        def _(act):
            a = nc.scalar
            start(act, 2)
            with nc.allow_non_contiguous_dma(reason="small per-head vectors, once"):
                act.dma_start(g_t, ln_g.rearrange("h l -> l h")).then_inc(s["g_in"], 16)
                act.dma_start(b_t, ln_b.rearrange("h l -> l h")).then_inc(s["g_in"], 16)
            act.dma_start(gw_raw[:], gate_w.rearrange("(k p) e -> p k e", p=P)).then_inc(s["g_in"], 16)
            act.dma_start(gb_bc[:], gate_b.partition_broadcast(P)).then_inc(s["g_in"], 16)
            act.dma_start(bo_bc[:], bo.partition_broadcast(P)).then_inc(s["g_in"], 16)
            act.dma_start(eb_bc[:], expert_b.partition_broadcast(P)).then_inc(s["g_in"], 16)
            for k in range(KB):
                act.wait_ge(s["wot_ps"], count(k + 1))
                a.activation(wo_t[:, k, :], PS[:, k, :], ACT.Copy).then_inc(s["wot_done"], 1)
            for k in range(KB):
                act.wait_ge(s["comb_ps"], count(k + 1))
                a.activation(comb[:, k, :], PS[:, 4 + k, :], ACT.Copy).then_inc(s["comb_done"], 1)
            with act.Fori(0, NC) as i:
                for u in range(B):
                    n = i * B + u
                    act.wait_ge(s["mv_done"], count(n + 1))
                    a.activation(sd4[:], mv[:, :, 1], ACT.Sqrt, bias=eps[:]).then_inc(s["sd4_done"], 1)
                    act.wait_ge(s["xr_done"], count(n * KB))
                    for k in range(KB):
                        act.wait_ge(s["tp_ps"], count(n * KB + k + 1))
                        a.activation(x_t[:, k, :], PS[:, k, :], ACT.Copy).then_inc(s["xt_done"], 1)
                    for k in range(KB):
                        act.wait_ge(s["xt_done"], count(n * KB + k + 1))
                        a.activation(xhl[:, :, k, 0, :], x_t[:, k, :].rearrange("p (t c) -> p t c", t=CT),
                                     ACT.Copy).then_inc(s["xh_done"], 1)
                    act.wait_ge(s["stored"], count(n * 16 * STORES_A))
                    for k in range(KB):
                        act.wait_ge(s["q_ps"], count(n * KB + k + 1))
                        a.activation(q_hi[:, k, :], PS[:, k, :], ACT.Copy).then_inc(s["qh_done"], 1)
                    act.wait_ge(s["var_ps"], count(n + 1))
                    a.activation(sd_buf, PS[0:H, 4, :], ACT.Sqrt, bias=eps[0:H, :]).then_inc(s["sd_done"], 1)
                    for k in range(KB):
                        act.wait_ge(s["k_ps"], count(n * KB + k + 1))
                        a.activation(k_hi[:, k, :], PS[:, k, :], ACT.Identity, bias=bk[:, k:k + 1]).then_inc(s["kh_done"], 1)
            def max_row(sh, w, c):
                act.wait_ge(s["m_ps"], count(sh * NC + c + 1))
                a.activation(q_st[w][3 * HD:3 * HD + 1, c * CH:(c + 1) * CH], PS[3 * HD:3 * HD + 1, 7, :],
                             ACT.Copy).then_inc(s["m_done"], 1)

            def heads(it, more):
                for kk in range(2 * NU + PV_LAG):
                    if kk < 2 * NU:
                        c, j, (wa, wb), off, _m = UNITS[kk % NU]
                        act.wait_ge(s["s2_ps"], count(it * (2 * NU) + kk + 1))
                        act.wait_ge(s["pv_done"], count(it * (2 * NU) + kk - 3))
                        z = PS[:, 2 + 2 * (kk % 2):4 + 2 * (kk % 2), :].rearrange("p a s -> p (a s)")
                        a.activation(probs[kk % 4][:, 0:off + wb], z[:, 0:off + wb], ACT.Exp,
                                     scale=SCALE).then_inc(s["exp_done"], 1)
                        u, k = divmod(kk, NU)
                        for ahead, cc in slot_max_rows(k):
                            if u + ahead < 2 or more:
                                max_row(it * 2 + u + ahead, (u + ahead) % 2, cc)
                    pk = kk - PV_LAG
                    if pk >= 0 and pk % NU in LAST:
                        q = (pk // NU) * NC + LAST[pk % NU]
                        act.wait_ge(s["pv_done"], count(it * (2 * NU) + pk + 1))
                        act.wait_ge(s["tr_ps"], count(it * (2 * NC) + q - 1))
                        a.activation(ot[q % 2][0:2 * HD + V1, :], PS[0:2 * HD + V1, 6, :], ACT.Copy).then_inc(s["ot_done"], 1)

            for c in range(NC - 1):
                max_row(0, 0, c)
            with act.Fori(0, BH // 2 - 1) as it:
                heads(it, True)
            heads(BH // 2 - 1, False)
            def hi(n, u):
                act.wait_ge(s["gt_ps"], count(n + 1))
                act.wait_ge(s["z_ps"], count(n - 1))
                a.activation(xg_hi[u].rearrange("p k c -> p (k c)"), PS[:, 4 + u, :], ACT.Copy).then_inc(s["gh_done"], 1)

            def experts(i, more):
                for u in range(2):
                    n = i * 2 + u
                    if u == 0 or more:
                        hi(n + 1, 1 - u)
                    act.wait_ge(s["z_done"], count(n + 1))
                    act.wait_ge(s[f"y_st{u}"], count(i * 16))
                    a.activation(y_sb[u], z_sb[u], ACT.Relu, scale=1.0 / TOP).then_inc(s["y_done"], 1)

            hi(0, 0)
            with act.Fori(0, PT // 2 - 1) as i:
                experts(i, True)
            experts(PT // 2 - 1, False)

            def heads_of(i, u, n):
                act.wait_ge(s["otp_ps"], count(n - 1))
                a.activation(o_in[u].rearrange("p (h d) -> p h d", h=H),
                             attn[:, ds(i, 1), u * H:(u + 1) * H, :].rearrange("p t h d -> p (t h) d"),
                             ACT.Copy).then_inc(s["o_done"], 1)

            def outs(i, more):
                for u in range(B):
                    n = i * B + u
                    if u == 0 or more:
                        heads_of(i + u, 1 - u, n + 1)
                    act.wait_ge(s["otp_ps"], count(n + 1))
                    act.wait_ge(s["proj_ps"], count(n - 1))
                    a.activation(o_t[u].rearrange("p k c -> p (k c)"), PS[:, 6 + u, :], ACT.Copy).then_inc(s["otc_done"], 1)

            heads_of(0, 0, 0)
            with act.Fori(0, ST - 1) as i:
                outs(i, True)
            outs(ST - 1, False)

        @block.vector
        def _(dve):
            v = nc.vector
            start(dve, 3)
            link, n0 = linker(dve, s["dve0"])
            dve.wait_ge(s["g_in"], count(96))
            dve.wait_ge(s["w_in"], count(64))

            def per_head(t):
                return t.rearrange("p (h d) -> p h d", h=H)
            for w, r in ((wuk, gwuk), (wuv, gwuv)):
                last = v.tensor_tensor(per_head(r), per_head(w), g_t.unsqueeze(2).to_broadcast([P, H, HD]), ALU.mult)
            last.then_inc(s["gw_done"], 1)
            link(v.tensor_scalar(gw_raw[:], gw_raw[:], WS, None, ALU.mult))
            link(v.tensor_copy(gw_hl[:, 0], gw_raw[:]))
            v.tensor_tensor(gw_hl[:, 1], gw_raw[:], gw_hl[:, 0], ALU.subtract).then_inc(s["gates_done"], 1)
            dve.wait_ge(s["wc_ps"], count(1))
            v.tensor_copy(wc, PS[:, 0, :]).then_inc(s["wc_done"], 1)
            dve.wait_ge(s["fold_ps"], count(1))
            for b, bd in ((1, bdk), (2, bdg), (3, bdv)):
                for j in range(HK):
                    r = slice(HD * j, HD * (j + 1))
                    last = v.tensor_copy(bd[r, :, r], PS[r, b, 0:P].rearrange("p (k c) -> p k c", k=KB))
            v.tensor_copy(bk[:], PS[:, 4, 0:KB])
            v.tensor_copy(bv_bc[:], PS[:, 5, :]).then_inc(s["fold_done"], 1)
            dve.wait_ge(s["consts"], count(1))
            link(v.memset(v_st[:, :, :, HD:V1], 1.0))
            with dve.Fori(0, NC) as i:
                for u in range(B):
                    n = i * B + u
                    lnk, cnt = linker(dve, s["dveA"], n * A_LINKS)
                    dve.wait_ge(s[f"x_in{u}"], count((i + 1) * 16))
                    for t in range(CT):
                        v.bn_stats(stats[:, t, :], x_in[u][:, t, :])
                    v.drain()
                    for t in range(CT):
                        last = v.bn_aggr(mv[:, t, :], stats[:, t, :])
                    last.then_inc(s["mv_done"], 1)
                    dve.wait_ge(s["sd4_done"], count(n + 1))
                    lnk(v.reciprocal(rs4[:], sd4[:]))
                    dve.wait_ge(s["tp_ps"], count(n * KB))
                    dve.wait_ge(s["xn_st"], count(n * 16))
                    for t in range(CT):
                        v.tensor_scalar(xn[:, t, :], x_in[u][:, t, :], mv[:, t, 0:1], rs4[:, t:t + 1],
                                        ALU.subtract, ALU.mult).then_inc(s["xn_done"], 1)
                    for k in range(KB):
                        dve.wait_ge(s["xh_done"], count(n * KB + k + 1))
                        v.tensor_tensor(xhl[:, :, k, 1, :], x_t[:, k, :].rearrange("p (t c) -> p t c", t=CT),
                                        xhl[:, :, k, 0, :], ALU.subtract).then_inc(s["xl_done"], 1)
                    for k in range(KB):
                        dve.wait_ge(s["y_ps"], count(n * KB + k + 1))
                        v.tensor_tensor(prod[:, k, :], PS[:, 4 + k, :], x_t[:, k, :], ALU.mult).then_inc(s["prod_done"], 1)
                    for k in range(KB):
                        dve.wait_ge(s["qh_done"], count(n * KB + k + 1))
                        v.tensor_tensor(q_lo[:, k, :], PS[:, k, :], q_hi[:, k, :], ALU.subtract).then_inc(s["ql_done"], 1)
                    dve.wait_ge(s["lg_ps"], count(n + 1))
                    ins = v.scalar_tensor_tensor(out=lg[:], in0=PS[:, 5, 0:CT * NE].rearrange("p (t e) -> p t e", t=CT),
                                                 scalar=1.0 / WS, in1=gb_bc[:].unsqueeze(1).to_broadcast([P, CT, NE]),
                                                 op0=ALU.mult, op1=ALU.add)
                    ins.then_inc(s["lg_done"], 1)
                    dve.wait_ge(s["sd_done"], count(n + 1))
                    v.reciprocal(rs_row, sd_buf).then_inc(s["rs_done"], 1)
                    v.drain()
                    for t in range(CT):
                        v.max(top8[:, t, :], lg[:, t, :])
                    v.drain()
                    for t in range(CT):
                        v.max_index(idx8[:, t, :], top8[:, t, :], lg[:, t, :])
                    v.drain()
                    lnk(v.tensor_copy(idxf[:], idx8[:]))
                    for k in range(TOP):
                        v.tensor_tensor(chosen[:, k, ds(i * CT + u * ST, CT), :],
                                        iota[:, 0:NE].unsqueeze(1).to_broadcast([P, CT, NE]),
                                        idxf[:, :, k:k + 1].to_broadcast([P, CT, NE]), ALU.is_equal)
                    for k in range(KB):
                        dve.wait_ge(s["rb_ps"], count(n * KB + k + 1))
                        v.tensor_tensor(xr[:, k, :], PS[:, 4 + k, :], x_t[:, k, :], ALU.mult).then_inc(s["xr_done"], 1)
                    for k in range(KB):
                        dve.wait_ge(s["kh_done"], count(n * KB + k + 1))
                        v.scalar_tensor_tensor(out=k_lo[:, k, :], in0=PS[:, k, :], scalar=bk[:, k:k + 1],
                                               in1=k_hi[:, k, :], op0=ALU.add, op1=ALU.subtract).then_inc(s["kl_done"], 1)
                    for k in range(KB):
                        dve.wait_ge(s["vv_ps"], count(n * KB + k + 1))
                        v.tensor_tensor(v_st[:, HK * k:HK * (k + 1), :, 0:HD].rearrange("p h t d -> p t h d"),
                                        PS[:, 4 + k, :].rearrange("p (t h d) -> p t h d", t=CT, h=HK),
                                        bv_bc[:, k * P:(k + 1) * P].rearrange("p (h d) -> p h d", h=HK)
                                        .unsqueeze(1).to_broadcast([P, CT, HK, HD]), ALU.add).then_inc(s["v_done"], 1)
                    assert cnt[0] == A_LINKS, cnt
            dve.wait_ge(s["stage_free"], count(B * NC))
            dve.wait_ge(s["stored"], count(16 * STORES_A * B * NC))
            for w in range(2):
                v.memset(k_st[w][3 * HD:3 * HD + 1, :], -MS)
            v.memset(pm[:], LOWEST)
            v.memset(PS[:, 6, :], 0.0).then_inc(s["b_zero"], 1)
            dve.wait_ge(s["b_zero"], count(1))
            dve.wait_ge(s["xn_st"], count(16 * B * NC))
            lnk, cnt = linker(dve, s["dveR"])
            v.memset(ones16, 1.0)
            v.memset(r_ones, 1.0)
            v.memset(r_exp, 0.0)
            v.tensor_tensor(r_m16.rearrange("p (g e) -> p g e", e=NE), chosen[:, 0], chosen[:, 1], ALU.add).then_inc(s["counted"], 1)
            dve.wait_ge(s["cnt_ps"], count(1))
            ge, eg = "p (g e) -> p g e", "p (e g) -> p e g"
            v.tensor_copy(r_in, PS[:, 0, 0:NT * NE])
            v.tensor_copy(r_tot.rearrange(eg, e=NE), PS[:, 1, 0:NT * NE].rearrange("p (g e) -> p e g", e=NE)).then_inc(s["cnt_done"], 1)
            dve.wait_ge(s["cnt_done"], count(1))
            for e in range(NE):
                c = slice(e * NT, (e + 1) * NT)
                last = v.tensor_tensor_scan(r_incl[:, c], r_ones, r_tot[:, c], 0.0, ALU.mult, ALU.add)
            lnk(last)
            lnk(v.tensor_scalar(r_n, r_incl.rearrange(eg, e=NE)[:, :, NT - 1], float(P - 1), None, ALU.add))
            lnk(v.tensor_copy(r_int[:, 0:NE], r_n))
            lnk(v.tensor_scalar(r_int2[:, 0:NE], r_int[:, 0:NE], 7, None, ALU.arith_shift_right))
            lnk(v.tensor_copy(r_tiles, r_int2[:, 0:NE]))
            lnk(v.tensor_tensor_scan(r_cum, r_ones[:, 0:NE], r_tiles, 0.0, ALU.mult, ALU.add))
            lnk(v.tensor_tensor(r_base, r_cum, r_tiles, ALU.subtract))
            lnk(v.tensor_scalar(r_base, r_base, float(P), None, ALU.mult))
            lnk(v.tensor_tensor(r_incl, r_incl, r_tot, ALU.subtract))
            lnk(v.tensor_tensor(r_incl.rearrange(eg, e=NE), r_incl.rearrange(eg, e=NE),
                                r_base.unsqueeze(2).to_broadcast([P, NE, NT]), ALU.add))
            lnk(v.tensor_tensor(r_slot.rearrange(ge, e=NE), r_in.rearrange(ge, e=NE),
                                r_incl.rearrange("p (e g) -> p g e", e=NE), ALU.add))
            for k in range(TOP):
                lnk(v.tensor_tensor(r_tmp.rearrange(ge, e=NE), chosen[:, k], r_slot.rearrange(ge, e=NE), ALU.mult))
                lnk(v.reduce_sum(r_f[:, k * NT:(k + 1) * NT], r_tmp.rearrange(ge, e=NE), AX))
            v.tensor_copy(place[:].rearrange("p k g -> p (k g)"), r_f)
            lnk(v.tensor_copy(r_int, r_f))
            lnk(v.tensor_scalar(r_int2, r_int, P - 1, None, ALU.bitwise_and))
            lnk(v.tensor_copy(r_tmp[:, 0:NT * TOP], r_int2))
            lnk(v.tensor_scalar(r_int2, r_int, 7, None, ALU.arith_shift_right))
            lnk(v.tensor_copy(r_f, r_int2))
            v.scalar_tensor_tensor(out=place_at[:].rearrange("p k g -> p (k g)"), in0=r_tmp[:, 0:NT * TOP], scalar=float(PT),
                                   in1=r_f, op0=ALU.mult, op1=ALU.add)
            for e in range(NE):
                lnk(v.scalar_tensor_tensor(out=r_exp, in0=iota[:], scalar=r_cum[:, e:e + 1], in1=r_exp,
                                           op0=ALU.is_ge, op1=ALU.add))
            v.tensor_scalar(expert_of[:], r_exp, float(NE - 1), None, ALU.min).then_inc(s["placed"], 1)
            dve.wait_ge(s["placed"], count(1))

            def piece(sh, n):
                i, p, w = PIECES[n]
                c, r = divmod(i, CT)
                seq = sh * NP_ + n
                dve.wait_ge(s["s1_ps"], count(seq + 1))
                bank = n % 2
                if p < i // CT:
                    ins = v.reduce_max(pm[:, c, r, p:p + 1], PS[:, bank, 0:w], AX)
                else:
                    v.reduce_max(pm[:, c, r, p:p + 1], PS[:, bank, 0:w - P + 1], AX)
                    ins = v.tensor_tensor_reduce(out=junk[:, r, :], in0=PS[:, bank, w - P:w], in1=tri[:], scale=1.0,
                                                 scalar=LOWEST, op0=ALU.add, op1=ALU.max,
                                                 accum_out=pm[:, c, r, PMS - 1:PMS])
                ins.then_inc(s["s1_done"], 1)
                if n in CHUNK_END:
                    dve.wait_ge(s["s1_done"], count(seq + 1))
                    v.reduce_max(mx[:, c, :], pm[:, c, :, :], AX).then_inc(s["mx_done"], 1)
                    dve.wait_ge(s["mx_done"], count((sh * NC + c) * 2 + 1))
                    v.tensor_scalar(mx16[:, c, :], mx[:, c, :], 1.0 / MS, None, ALU.mult).then_inc(s["mx_done"], 1)

            def norm(it, q):
                lnk, cnt = linker(dve, s["dveB"], (it * (2 * NC) + q) * 3)
                dve.wait_ge(s["tr_ps"], count(it * (2 * NC) + q + 1))
                T = PS[:, 7, 0:CT * (2 * HD + V1)].rearrange("p (t f) -> p t f", t=CT)
                dve.wait_ge(s["norm_done"], count(it * (2 * NC) + q))
                lnk(v.tensor_copy(half_b[:], T[:, :, 2 * HD:2 * HD + V1]))
                lnk(v.tensor_tensor(whole[:], T[:, :, 0:V1], half_b[:], ALU.add))
                lnk(v.reciprocal(rden[:], whole[:, :, HD:V1]))
                u, c = divmod(q, NC)
                v.tensor_tensor(attn[:, CT * c:CT * (c + 1), ds(it * 2 + u, 1), :].rearrange("p t o d -> p t (o d)"),
                                whole[:, :, 0:HD], rden[:].to_broadcast([P, CT, HD]), ALU.mult).then_inc(s["norm_done"], 1)

            def heads(it, more):
                for kk in range(2 * NU + PV_LAG + 1):
                    u, k = divmod(kk, NU)
                    if kk < 2 * NU:
                        for ahead, n in slot_pieces(k):
                            if u + ahead < 2 or more:
                                piece(it * 2 + u + ahead, n)
                    pk = kk - PV_LAG - 1
                    if pk >= 0 and pk % NU in LAST:
                        norm(it, (pk // NU) * NC + LAST[pk % NU])

            for n in range(EARLY):
                piece(0, n)
            with dve.Fori(0, BH // 2 - 1) as it:
                heads(it, True)
            heads(BH // 2 - 1, False)
            def lo(n, u):
                dve.wait_ge(s["gh_done"], count(n + 1))
                v.tensor_tensor(xg_lo[u].rearrange("p k c -> p (k c)"), PS[:, 4 + u, :],
                                xg_hi[u].rearrange("p k c -> p (k c)"), ALU.subtract).then_inc(s["gl_done"], 1)

            def experts(i, more):
                for u in range(2):
                    n = i * 2 + u
                    if u == 0 or more:
                        lo(n + 1, 1 - u)
                    e = dve.value_load(expert_of[0:1, ds(n, 1)], min_val=0, max_val=NE - 1)
                    dve.wait_ge(s["z_ps"], count(n + 1))
                    dve.wait_ge(s["y_done"], count(n - 1))
                    v.scalar_tensor_tensor(out=z_sb[u], in0=PS[:, u, :], scalar=1.0 / WS,
                                           in1=eb_bc[:, ds(e, 1), :].rearrange("p e c -> p (e c)"),
                                           op0=ALU.mult, op1=ALU.add).then_inc(s["z_done"], 1)

            lo(0, 0)
            with dve.Fori(0, PT // 2 - 1) as i:
                experts(i, True)
            experts(PT // 2 - 1, False)
            with dve.Fori(0, ST) as i:
                for u in range(B):
                    n = i * B + u
                    lnk, cnt = linker(dve, s["dveE"], n * 3)
                    dve.wait_ge(s[f"out_done{u}"], count(i * 16))
                    dve.wait_ge(s[f"xc_in{u}"], count((i + 1) * 16))
                    dve.wait_ge(s["proj_ps"], count(n + 1))
                    lnk(v.tensor_tensor(acc[u], PS[:, 4 + u, :], xc[u], ALU.add))
                    lnk(v.tensor_tensor(acc[u], acc[u], bo_bc[:], ALU.add))
                    dve.wait_ge(s[f"yg_in{u}"], (i + 1) * (16 * TOP))
                    lnk(v.tensor_tensor(acc[u], acc[u], y_g[u][0], ALU.add))
                    v.tensor_tensor(acc[u], acc[u], y_g[u][1], ALU.add).then_inc(s["acc_done"], 1)

        @block.tensor
        def _(pe):
            t = nc.tensor
            start(pe, 4)
            pe.wait_ge(s["consts"], count(1))
            pe.wait_ge(s["w_in"], count(64))
            t.matmul(PS[:, 0, :], center, wdkv, start=True, stop=True).then_inc(s["wc_ps"], 1)
            pe.wait_ge(s["g_in"], count(96))
            pe.wait_ge(s["wc_done"], count(1))
            pe.wait_ge(s["gw_done"], count(1))
            for h in range(H):
                k, j = divmod(h, HK)
                o = slice(HD * j, HD * (j + 1))
                c = slice(HD * h, HD * (h + 1))
                f = slice(HD * k, HD * (k + 1))
                t.matmul(PS[o, 1, f], wc[:, c], gwuk[:, c], start=True, stop=True)
                t.matmul(PS[o, 2, f], wc[:, c], wc[:, c], start=True, stop=True)
                t.matmul(PS[o, 3, f], wc[:, c], gwuv[:, c], start=True, stop=True)
                t.matmul(PS[o, 4, k:k + 1], wuk[:, c], b_t[:, h:h + 1], start=True, stop=True)
                last = t.matmul(PS[:, 5, c], b_t[:, h:h + 1].to_broadcast([P, P]), wuv[:, c], start=True, stop=True)
            last.then_inc(s["fold_ps"], 1)
            pe.wait_ge(s["fold_done"], count(1))
            for k in range(KB):
                for n in range(4):
                    last = t.transpose(PS[:, k, n * P:(n + 1) * P], wo_raw[:, n, k * P:(k + 1) * P], ident[:])
                last.then_inc(s["wot_ps"], 1)
            pe.wait_ge(s["wqo_in"], count(16 * 2 * HK))
            for k in range(KB):
                pe.wait_ge(s["wot_done"], count(k + 1))
                t.matmul(PS[:, 4 + k, :], bdo[:, k, :], wo_t[:, k, :], start=True, stop=True).then_inc(s["comb_ps"], 1)
            pe.wait_ge(s["comb_done"], count(KB))
            pe.wait_ge(s["gates_done"], count(1))
            with pe.Fori(0, NC) as i:
                for u in range(B):
                    n = i * B + u
                    for tl in range(CT):
                        pe.wait_ge(s["xn_done"], count(n * CT + tl + 1))
                        if tl == 0:
                            pe.wait_ge(s["kl_done"], count(n * KB))
                        for k in range(KB):
                            last = t.transpose(PS[:, k, tl * P:(tl + 1) * P], xn[:, tl, k * P:(k + 1) * P], ident[:])
                            if tl == CT - 1:
                                last.then_inc(s["tp_ps"], 1)
                    pe.wait_ge(s["v_done"], count(n * KB))
                    for k in range(KB):
                        pe.wait_ge(s["xt_done"], count(n * KB + k + 1))
                        t.matmul(PS[:, 4 + k, :], bdg[:, k, :], x_t[:, k, :], start=True, stop=True).then_inc(s["y_ps"], 1)
                        t.matmul(PS[:, k, :], bdq[:, k, :], x_t[:, k, :], start=True, stop=True).then_inc(s["q_ps"], 1)
                    pe.wait_ge(s["prod_done"], count(n * KB + KB))
                    pe.wait_ge(s["xl_done"], count(n * KB + KB))
                    for tl in range(CT):
                        terms = [(k, z, y) for k in range(KB) for z in range(2) for y in range(2)]
                        for q, (k, z, y) in enumerate(terms):
                            last = t.matmul(PS[:, 5, tl * NE:(tl + 1) * NE], xhl[:, tl, k, z, :], gw_hl[:, y, k, :],
                                            start=q == 0, stop=q == len(terms) - 1)
                    last.then_inc(s["lg_ps"], 1)
                    for k in range(KB):
                        last = t.matmul(PS[0:H, 4, :], head_of[:, k, :], prod[:, k, :], start=k == 0, stop=k == KB - 1)
                    last.then_inc(s["var_ps"], 1)
                    pe.wait_ge(s["rs_done"], count(n + 1))
                    pe.wait_ge(s["lg_done"], count(n + 1))
                    for k in range(KB):
                        t.matmul(PS[:, 4 + k, :], of_head[:, k * P:(k + 1) * P], rs_row, start=True,
                                 stop=True).then_inc(s["rb_ps"], 1)
                    for k in range(KB):
                        pe.wait_ge(s["xr_done"], count(n * KB + k + 1))
                        pe.wait_ge(s["ql_done"], count(n * KB + k + 1))
                        t.matmul(PS[:, k, :], bdk[:, k, :], xr[:, k, :], start=True, stop=True).then_inc(s["k_ps"], 1)
                        for tl in range(CT):
                            last = t.matmul(PS[:, 4 + k, tl * P:(tl + 1) * P], xr[:, k, tl * P:(tl + 1) * P],
                                            bdv[:, k, :], start=True, stop=True)
                        last.then_inc(s["vv_ps"], 1)
            pe.wait_ge(s["kl_done"], count(B * NC * KB))
            pe.wait_ge(s["v_done"], count(B * NC * KB))
            pe.wait_ge(s["b_zero"], count(1))
            pe.wait_ge(s["counted"], count(1))
            t.matmul(PS[:, 0, 0:NT * NE], upper[:], r_m16, start=True, stop=True)
            t.matmul(PS[:, 1, 0:NT * NE], ones16, r_m16, start=True, stop=True).then_inc(s["cnt_ps"], 1)
            pe.wait_ge(s["cnt_done"], count(1))

            def piece(sh, w, n, first):
                i, p, wd = PIECES[n]
                if not (first and n < 2):
                    pe.wait_ge(s["s1_done"], count(sh * NP_ + n - 1))
                t.matmul(PS[:, n % 2, 0:wd], q_st[w][0:3 * HD, i * P:(i + 1) * P], k_st[w][0:3 * HD, p * CH:p * CH + wd],
                         start=True, stop=True).then_inc(s["s1_ps"], 1)

            def max_row(sh, w, c, normed):
                pe.wait_ge(s["mx_done"], count((sh * NC + c + 1) * 2))
                pe.wait_ge(s["norm_done"], count(normed))
                pe.wait_ge(s["m_done"], count(sh * NC + c))
                for r in range(CT):
                    last = t.matmul(PS[3 * HD:3 * HD + 1, 7, r * P:(r + 1) * P], mx16[:, c, r:r + 1], ident16[:],
                                    start=True, stop=True)
                last.then_inc(s["m_ps"], 1)

            def heads(it, more):
                made = 0
                rows = 0
                for kk in range(2 * NU + PV_LAG + 1):
                    u, k = divmod(kk, NU)
                    if kk < 2 * NU:
                        c, j, wds, off, diag = UNITS[k]
                        pe.wait_ge(s["exp_done"], count(it * (2 * NU) + kk - 1))
                        if k in FIRST:
                            pe.wait_ge(s["m_done"], count((it * 2 + u) * NC + c + 1))
                        z = PS[:, 2 + 2 * (kk % 2):4 + 2 * (kk % 2), :].rearrange("p a s -> p (a s)")
                        beside = [(ahead, n) for ahead, n in slot_pieces(k) if u + ahead < 2 or more]
                        if k == S1_FROM and beside:
                            pe.wait_ge(s[f"ld{1 - u}"], count((it + 1 + u) * LOADS))
                        for a in range(2):
                            at = a * off
                            last = t.matmul(z[:, at:at + wds[a]], k_st[u][0:3 * HD + 1, (j + a) * P:(j + a + 1) * P],
                                            q_st[u][0:3 * HD + 1, (c + 1) * CH - wds[a]:(c + 1) * CH],
                                            start=True, stop=not diag)
                            if diag:
                                wm = 2 * P if (c, j, a) == (0, 0, 1) else P
                                last = t.matmul(z[:, at:at + wm], deny[:], later[:, int(wm > P), 0:wm], start=False, stop=True)
                            if a == 0 and beside:
                                ahead, n = beside[0]
                                piece(it * 2 + u + ahead, (u + ahead) % 2, n, False)
                        last.then_inc(s["s2_ps"], 1)
                    else:
                        beside = []
                    pk = kk - PV_LAG
                    piece_first = 0 <= pk < 2 * NU and pk % NU in FIRST
                    if beside and piece_first:
                        ahead, n = beside[1]
                        piece(it * 2 + u + ahead, (u + ahead) % 2, n, False)
                    if 0 <= pk < 2 * NU:
                        pu, p_ = divmod(pk, NU)
                        c, j, wds, off, _m = UNITS[p_]
                        pe.wait_ge(s["exp_done"], count(it * (2 * NU) + pk + 1))
                        if p_ in FIRST:
                            pe.wait_ge(s["ot_done"], count(it * (2 * NC) + pu * NC + c))
                        for a in range(2):
                            rows_ = slice(2 * HD * a, 2 * HD * a + V1)
                            last = t.matmul(PS[rows_, 6, CH - wds[a]:CH], v_sb[pu][:, j + a, :],
                                            probs[pk % 4][:, a * off:a * off + wds[a]],
                                            start=p_ in FIRST, stop=p_ in LAST)
                        last.then_inc(s["pv_done"], 1)
                    if beside and not piece_first:
                        ahead, n = beside[1]
                        piece(it * 2 + u + ahead, (u + ahead) % 2, n, False)
                    if kk < 2 * NU:
                        for ahead, cc in slot_max_rows(k):
                            if u + ahead < 2 or more:
                                max_row(it * 2 + u + ahead, (u + ahead) % 2, cc, it * (2 * NC) + made)
                                rows += 1
                    tk = kk - PV_LAG - 1
                    if tk >= 0 and tk % NU in LAST:
                        q = (tk // NU) * NC + LAST[tk % NU]
                        pe.wait_ge(s["ot_done"], count(it * (2 * NC) + q + 1))
                        pe.wait_ge(s["norm_done"], count(it * (2 * NC) + q))
                        pe.wait_ge(s["m_done"], count(it * (2 * NC) + NC - 1 + rows))
                        for r in range(CT):
                            W_ = 2 * HD + V1
                            last = t.transpose(PS[:, 7, r * W_:(r + 1) * W_], ot[q % 2][0:W_, r * P:(r + 1) * P], ident[0:W_, 0:W_])
                        last.then_inc(s["tr_ps"], 1)
                        made += 1

            LOADS = 7 * 16
            pe.wait_ge(s["ld0"], count(LOADS))
            for n in range(EARLY):
                piece(0, 0, n, True)
                if n in CHUNK_END:
                    max_row(0, 0, CHUNK_END[n], 0)
            with pe.Fori(0, BH // 2 - 1) as it:
                heads(it, True)
            heads(BH // 2 - 1, False)
            pe.wait_ge(s["norm_done"], count(NC * BH))

            def turn(n, i, u):
                pe.wait_ge(s[f"xg_in{u}"], (i + 1) * 16)
                pe.wait_ge(s["gl_done"], count(n - 1))
                for k in range(KB):
                    last = t.transpose(PS[:, 4 + u, k * P:(k + 1) * P], x_g[u][:, k * P:(k + 1) * P], ident[:])
                last.then_inc(s["gt_ps"], 1)

            def experts(i, more):
                for u in range(2):
                    n = i * 2 + u
                    if u == 0 or more:
                        turn(n + 1, i + u, 1 - u)
                    e = pe.value_load(expert_of[0:1, ds(n, 1)], min_val=0, max_val=NE - 1)
                    pe.wait_ge(s["gl_done"], count(n + 1))
                    pe.wait_ge(s["z_done"], count(n - 1))
                    terms = [(k, x_, w) for k in range(KB) for x_, w in ((xg_hi, w_hi), (xg_lo, w_hi), (xg_hi, w_lo))]
                    for q, (k, x_, w) in enumerate(terms):
                        last = t.matmul(PS[:, u, :], x_[u][:, k, :], w[:, ds(e, 1), k * E:(k + 1) * E].rearrange("p e c -> p (e c)"),
                                        start=q == 0, stop=q == len(terms) - 1)
                    last.then_inc(s["z_ps"], 1)

            turn(0, 0, 0)
            with pe.Fori(0, PT // 2 - 1) as i:
                experts(i, True)
            experts(PT // 2 - 1, False)

            def turn_heads(n, u):
                pe.wait_ge(s["o_done"], count(n + 1))
                pe.wait_ge(s["otc_done"], count(n - 1))
                for k in range(KB):
                    last = t.transpose(PS[:, 6 + u, k * P:(k + 1) * P], o_in[u][:, k * P:(k + 1) * P], ident[:])
                last.then_inc(s["otp_ps"], 1)

            def outs(i, more):
                for u in range(B):
                    n = i * B + u
                    if u == 0 or more:
                        turn_heads(n + 1, 1 - u)
                    pe.wait_ge(s["otc_done"], count(n + 1))
                    pe.wait_ge(s["acc_done"], count(n - 1))
                    for k in range(KB):
                        last = t.matmul(PS[:, 4 + u, :], o_t[u][:, k, :], comb[:, k, :], start=k == 0, stop=k == KB - 1)
                    last.then_inc(s["proj_ps"], 1)

            turn_heads(0, 0)
            with pe.Fori(0, ST - 1) as i:
                outs(i, True)
            outs(ST - 1, False)


_INS = ["x", "Wq", "Wdkv", "Wuk", "Wuv", "ln_g", "ln_b", "Wo_h", "Wo", "bo", "gate_w", "gate_b", "expert_w", "expert_b"]


def kernel(L0_attn_x, L0_attn_Wq, L0_attn_Wdkv, L0_attn_Wuk, L0_attn_Wuv, L0_attn_ln_g, L0_attn_ln_b, L0_attn_Wo_h,
           L0_attn_Wo, L0_attn_bo, L0_ffn_gate_w, L0_ffn_gate_b, L0_ffn_expert_w, L0_ffn_expert_b):
    import numpy as _np
    import concourse.bacc as _bacc
    from concourse import mybir as _mybir
    from concourse.bass_utils import run_bass_kernel_spmd as _run

    given = [L0_attn_x, L0_attn_Wq, L0_attn_Wdkv, L0_attn_Wuk, L0_attn_Wuv, L0_attn_ln_g, L0_attn_ln_b, L0_attn_Wo_h,
             L0_attn_Wo, L0_attn_bo, L0_ffn_gate_w, L0_ffn_gate_b, L0_ffn_expert_w, L0_ffn_expert_b]
    nc = _bacc.Bacc("TRN2", target_bir_lowering=False, num_devices=1)
    arrays, args = {}, []
    for name, value in zip(_INS, given):
        a = _np.ascontiguousarray(value)
        arrays[f"in_{name}"] = a
        args.append(nc.dram_tensor(f"in_{name}", a.shape, _mybir.dt.from_np(a.dtype), kind="ExternalInput").ap())
    out = nc.dram_tensor("out_0", tuple(L0_attn_x.shape), _mybir.dt.float32, kind="ExternalOutput").ap()
    layer_kernel(nc, *args, out)
    r = _run(nc, [arrays], core_ids=[0])
    return r.results[0]["out_0"]
```

```python
import numpy as np
import concourse.bass as bass
from concourse import mybir
from contextlib import ExitStack


def layer_kernel(nc, x, Wq, Wdkv, Wuk, Wuv, ln_g, ln_b, Wo_h, Wo, bo,
                 gate_w, gate_b, expert_w, expert_b, out):
    f32, f16, u32, i32 = mybir.dt.float32, mybir.dt.float16, mybir.dt.uint32, mybir.dt.int32
    ALU, ACT, AX = mybir.AluOpType, mybir.ActivationFunctionType, mybir.AxisListType.X
    ds = bass.ds

    B, S, E = x.shape
    H, L, HD = Wdkv.shape
    NE = gate_w.shape[1]
    P = 128
    KB = E // P
    HK = P // HD
    CH = 512
    CT = CH // P
    NC = S // CH
    ST = S // P
    BH = B * H
    V1 = HD + 1
    SCALE = 1.0 / float(L) ** 0.5
    WS = 256.0
    TOP = 2
    NT = B * ST
    PT = -(-(NT * TOP + NE - 1) // 2) * 2
    MS = 64.0
    AHEAD_G = 4
    LOWEST = -3.0e38
    FAR = 32768.0
    EPS = 1e-5

    q_dram = nc.dram_tensor("q_pieces", (2, BH * HD, S), f16, kind="Internal").ap()
    k_dram = nc.dram_tensor("k_pieces", (2, BH * HD, S), f16, kind="Internal").ap()
    v_dram = nc.dram_tensor("v_rows", (BH, P, ST, V1), f32, kind="Internal").ap()
    xn_dram = nc.dram_tensor("xn_rows", (NT * P, 2 * E), f16, kind="Internal").ap()
    id_dram = nc.dram_tensor("token_of_place", (P * PT, 1), u32, kind="Internal").ap()
    y_dram = nc.dram_tensor("expert_rows", (PT * P, E), f32, kind="Internal").ap()

    ctx = ExitStack()
    with ctx:
        def sb(name, shape, dt):
            return ctx.enter_context(nc.sbuf_tensor(name, shape, dt))

        def sem(name):
            return ctx.enter_context(nc.semaphore(name))

        arena1 = sb("arena1", [P, 16384], f32)
        arena2 = sb("arena2", [P, 10304], f32)
        w_hi = sb("w_hi", [P, NE, KB * E], f16)
        w_lo = sb("w_lo", [P, NE, KB * E], f16)
        eb_bc = sb("eb_bc", [P, NE, E], f32)
        comb_hl = sb("comb_hl", [P, 2, KB, E], f16)
        bo_bc = sb("bo_bc", [P, E], f32)
        bv_bc = sb("bv_bc", [P, E], f32)
        ident = sb("ident", [P, P], f32)
        ident16 = sb("ident16", [P, P], f16)
        tri = sb("tri", [P, P], f32)
        bk = sb("bk", [P, KB], f32)
        gw_hl = sb("gw_hl", [P, KB, 2, NE], f16)
        gw_raw = sb("gw_raw", [P, KB, NE], f32)
        gb_bc = sb("gb_bc", [P, NE], f32)
        eps = sb("eps", [P, 1], f32)
        ws_col = sb("ws_col", [P, 1], f32)
        deny = sb("deny", [P, P], f16)
        later = sb("later", [P, 2, 2 * P], f16)
        iota = sb("iota", [P, PT], f32)
        chosen = sb("chosen", [P, TOP, NT, NE], f16)
        place = sb("place", [P, TOP, NT], u32)
        place_at = sb("place_at", [P, TOP, NT], u32)
        expert_of = sb("expert_of", [P, PT], i32)
        upper = sb("upper", [P, P], f16)
        zero_ids = sb("zero_ids", [P, PT], u32)
        token_id = sb("token_id", [P, NT], u32)
        cur = sb("cur", [P, 2 * TOP], u32)
        cur_id = sb("cur_id", [P, AHEAD_G], u32)
        ids = sb("ids", [P, PT], u32)
        x_g0 = sb("x_g0", [P, 2 * E], f16)

        def carve(arena):
            at = [0]

            def take(n, dt=f32):
                w = n if dt == f32 else n // 2
                a = arena[:, at[0]:at[0] + w]
                at[0] += w
                assert at[0] <= arena.shape[1], at[0]
                return a if dt == f32 else a.bitcast(dt)
            return take

        t0 = carve(arena1)
        t0(2 * CT * E)
        wdkv = t0(H * HD)
        wuk = t0(H * HD)
        wuv = t0(H * HD)
        wc = t0(H * HD)
        gwuk = t0(H * HD)
        gwuv = t0(H * HD)
        bwuv = t0(H * HD)
        ones = t0(P)
        bo_c = t0(KB)
        g_t = t0(H)
        b_t = t0(H)
        center = t0(P)
        bdo = t0(KB * P).rearrange("p (k c) -> p k c", k=KB)
        wo_raw = t0(4 * E).rearrange("p (n c) -> p n c", n=4)
        wo_t = t0(KB * E).rearrange("p (k c) -> p k c", k=KB)
        tA = carve(arena2)
        q_hi, q_lo, k_hi, k_lo = (tA(KB * CH, f16).rearrange("p (k s) -> p k s", k=KB) for _ in range(4))
        v_st = [tA(CT * H * V1).rearrange("p (h t f) -> p h t f", t=CT, h=H) for _ in range(2)]
        stage = [tA(E) for _ in range(2)]
        tA = carve(arena1)
        x_in = [tA(CT * E).rearrange("p (t c) -> p t c", t=CT) for _ in range(2)]
        xn = tA(CT * E).rearrange("p (t c) -> p t c", t=CT)
        x16 = tA(CT * 2 * E, f16).rearrange("p (t z c) -> p t z c", t=CT, z=2)
        xT = [tA(2 * KB * P, f16).rearrange("p (z k c) -> p z k c", z=2, k=KB) for _ in range(2)]
        xr = [tA(E) for _ in range(2)]
        xrT = [tA(KB * P).rearrange("p (k c) -> p k c", k=KB) for _ in range(2)]
        prod = tA(E)
        tA(E + 2 * P + 64)
        bdq_hl, bdg_hl = (tA(2 * KB * P, f16).rearrange("p (z k c) -> p z k c", z=2, k=KB) for _ in range(2))
        bdq, bdk, bdg, bdv = (tA(KB * P).rearrange("p (k c) -> p k c", k=KB) for _ in range(4))
        var, sd, rs = ([sb(f"{name}{u}", [P, H], f32) for u in range(2)] for name in ("var", "sd", "rs"))
        stats = sb("stats", [P, CT, 6], f32)
        mv = sb("mv", [P, CT, 2], f32)
        sd4 = sb("sd4", [P, CT], f32)
        rs4 = sb("rs4", [P, CT], f32)
        lg = sb("lg", [P, CT, NE], f32)
        top8 = sb("top8", [P, CT, 8], f32)
        idx8 = sb("idx8", [P, CT, 8], u32)
        idxf = sb("idxf", [P, CT, 8], f32)
        attn = arena1[:, :].rearrange("p (t g d) -> p t g d", t=ST, g=BH)
        tB = carve(arena2)
        probs = [tB(2 * CH) for _ in range(4)]
        q_st = [tB(S, f16) for _ in range(2)]
        k_st = [tB(S, f16) for _ in range(2)]
        v_sb = [tB(ST * V1).rearrange("p (j f) -> p j f", j=ST) for _ in range(2)]
        ot = [tB(CH) for _ in range(2)]
        PMS = 6
        pm = sb("pm", [P, NC, CT, PMS], f32)
        mx = sb("mx", [P, NC, CT], f32)
        mx16 = sb("mx16", [P, NC, CT], f16)
        half_b = sb("half_b", [P, CT, V1], f32)
        whole = sb("whole", [P, CT, V1], f32)
        rden = sb("rden", [P, CT, 1], f32)
        tR = carve(arena1)
        r_m16 = tR(NT * NE, f16)
        r_in, r_tot, r_incl, r_slot, r_tmp = (tR(NT * NE) for _ in range(5))
        r_n, r_tiles, r_cum, r_base = (tR(NE) for _ in range(4))
        r_int = tR(NT * TOP).bitcast(i32)
        r_int2 = tR(NT * TOP).bitcast(i32)
        r_f = tR(NT * TOP)
        r_exp = tR(PT)
        r_ones = tR(NT)
        ones16 = tR(P, f16)
        tD = carve(arena2)
        xg_T = [tD(2 * KB * P, f16).rearrange("p (z k c) -> p z k c", z=2, k=KB) for _ in range(2)]
        y_sb = [tD(E) for _ in range(2)]
        xc = [tD(E) for _ in range(B)]
        o16 = [tD(2 * E, f16).rearrange("p (z c) -> p z c", z=2) for _ in range(B)]
        oT = [tD(2 * KB * P, f16).rearrange("p (z k c) -> p z k c", z=2, k=KB) for _ in range(B)]
        acc = [tD(E) for _ in range(B)]
        y_g = [[tD(E) for _ in range(TOP)] for _ in range(B)]
        x_g = [x_g0[:, :]] + [y_g[q // 2][q % 2].bitcast(f16) for q in range(1, AHEAD_G)]
        junk = bv_bc[:, :].rearrange("p (r c) -> p r c", r=CT)

        PS = ctx.enter_context(nc.psum_tensor("PS", [P, 8, CH], f32))

        s = {n: sem(n) for n in (
            "eb_done w_in wqo_in g_in wo_in gate_in bias_in boc_done bob_ps bob_done zeroed consts wc_ps wc_done gw_done fold_ps fold_done bk_ps bk_done bv_ps bv_done "
            "wot_ps wot_done comb_ps comb_hi comb_done gates_done dve0 "
            "bd_done x_in0 x_in1 stage_in0 stage_in1 stage_free pool_link mv_done sd4_done xn_done xh_done xl_done tp_ps "
            "xt_done y_ps q_ps g_ps prod_done var_done sd_done rs_done xr_done tr2_ps xrt_done qh_done ql_done "
            "k_ps kh_done kl_done vv_ps v_done lg_done dve_rows dve_gates x_out0 x_out1 q_out0 q_out1 k_out0 k_out1 v_out0 v_out1 "
            "ld0 ld1 b_zero s1_ps s1_done mx_done m_ps m_done s2_ps exp_done pv_done ot_done tr_ps norm_done dveB "
            "counted cnt_ps cnt_done placed dveR id_zero id_done ids_in "
            "cur_done xg_in0 xg_in1 xg_in2 xg_in3 gt_ps gT_done z_ps half_done y_done y_st0 y_st1 "
            "xc_in0 xc_in1 o_hi_done o_lo_done otp_ps oT_done proj_ps yg_in0 yg_in1 gather_at acc_done out_done0 out_done1 dveE dve_z"
        ).split()}

        def linker(engine, semaphore, base=0):
            n = [0]

            def link(ins):
                n[0] += 1
                ins.then_inc(semaphore, 1)
                engine.wait_ge(semaphore, count(base + n[0]))
            return link, n

        START = 4
        FROM_ZERO = ("id_zero", "id_done", "ids_in", "xg_in0", "xg_in1", "xg_in2", "xg_in3",
                     "yg_in0", "yg_in1")

        def count(n):
            return n + START

        def start(engine, part):
            for semaphore in [s[name] for name in s if name not in FROM_ZERO][part::5]:
                engine.sem_inc(semaphore, START)

        def wait_stored(engine):
            for h in range(2):
                engine.wait_ge(s[f"q_out{h}"], count(16 * 2 * B * NC))
                engine.wait_ge(s[f"k_out{h}"], count(16 * 2 * B * NC))
                engine.wait_ge(s[f"x_out{h}"], count(16 * B * NC))
                engine.wait_ge(s[f"v_out{h}"], count(16 * NC))

        block = ctx.enter_context(nc.Block())

        x_v = x.rearrange("b (g p) d -> b p g d", p=P)
        q_v = q_dram.rearrange("z (b k r) s -> z b r k s", b=B, k=KB)
        k_v = k_dram.rearrange("z (b k r) s -> z b r k s", b=B, k=KB)
        v_v = v_dram.rearrange("(b h) r j f -> b r h (j f)", b=B)
        xn_v = xn_dram.rearrange("(b g p) d -> b p g d", b=B, p=P)
        ew_v = expert_w.rearrange("e (k p) o -> p e k o", p=P)
        out_v = out.rearrange("b (t p) d -> b t p d", p=P)
        xc_v = x.rearrange("b (t p) d -> b t p d", p=P)

        PER_IT = B * CT

        def ahead_tile(i, p, o, more):
            q = p + o
            if q < 0 or (q >= PER_IT and not more):
                return None
            ii = i + q // PER_IT
            q %= PER_IT
            return ii * PER_IT + q, q // CT, q % CT, ii

        def run_tiles(engine, step):
            for p in range(-ROWS_AHEAD, 0):
                step(0, p, True)
            with engine.Fori(0, NC - 1) as i:
                for p in range(PER_IT):
                    step(i, p, True)
            for p in range(PER_IT):
                step(NC - 1, p, False)

        QUERIES_AHEAD, TURN_AHEAD, ROWS_AHEAD = 2, 3, 4

        def head_units():
            units = []
            for c in range(NC):
                d0 = CT * c
                if c == 0:
                    own = [(c, 0, (CH, CH), CH, True), (c, 2, (2 * P, P), 2 * P, True)]
                    units += own
                    continue
                full = [(c, j, (CH, CH), CH, False) for j in range(0, d0, 2)]
                diag = [(c, d0, (CH, CH - P), CH, True), (c, d0 + 2, (2 * P, P), 2 * P, True)]
                units += full[:-1] + diag + full[-1:]
            return units

        UNITS = head_units()
        NU = len(UNITS)
        LAST = {max(k for k, un in enumerate(UNITS) if un[0] == c): c for c in range(NC)}
        FIRST = {min(k for k, un in enumerate(UNITS) if un[0] == c): c for c in range(NC)}
        PIECES = [(i, p, min(CH, P * (i + 1) - CH * p)) for i in range(ST) for p in range(i // CT + 1)]
        NP_ = len(PIECES)
        PV_LAG = 2
        S1_FROM = 5
        LEAD = range(PV_LAG + 1)
        SPAN = range(PV_LAG + 1, 2 * NU + PV_LAG + 1)
        EARLY = NP_ - 2 * S1_FROM

        def slot_pieces(k):
            if k < S1_FROM:
                return [(0, EARLY + 2 * k), (0, EARLY + 2 * k + 1)]
            return [(1, 2 * (k - S1_FROM)), (1, 2 * (k - S1_FROM) + 1)]

        CHUNK_END = {max(n for n, pc in enumerate(PIECES) if pc[0] // CT == c): c for c in range(NC)}

        def slot_max_rows(k):
            done = slot_pieces(k - 1) if k else []
            return [(ahead, CHUNK_END[n]) for ahead, n in done if n in CHUNK_END]

        assert 2 * (NU - S1_FROM) == EARLY and (NP_ - 1) // 2 * 2 + 1 == NP_ - 1

        def free_bank(kk):
            return 7 - UNITS[(kk - PV_LAG) % NU][0] % 2

        @block.sync
        def _(sp):
            start(sp, 0)
            sp.dma_start(wdkv.rearrange("p (h d) -> p h d", h=H), Wdkv.rearrange("h l d -> l h d")).then_inc(s["w_in"], 16)
            sp.dma_start(wuk.rearrange("p (h d) -> p h d", h=H), Wuk.rearrange("h l d -> l h d")).then_inc(s["w_in"], 16)
            sp.dma_start(wuv.rearrange("p (h d) -> p h d", h=H), Wuv.rearrange("h l d -> l h d")).then_inc(s["w_in"], 16)
            sp.wait_ge(s["zeroed"], count(1))
            for j in range(HK):
                r = slice(HD * j, HD * (j + 1))
                sp.dma_start(bdq[r, :, r], Wq.rearrange("(k j) i o -> j i k o", j=HK)[j]).then_inc(s["wqo_in"], 16)
                sp.dma_start(bdo[r, :, r], Wo_h.rearrange("(k j) e d -> j e k d", j=HK)[j]).then_inc(s["wqo_in"], 16)
            for u in range(B):
                sp.dma_start(x_in[u], x_v[u][:, 0:CT, :]).then_inc(s[f"x_in{u}"], 16)

            def step(i, p, more):
                at = ahead_tile(i, p, 1, more)
                if at:
                    n, u, tl, ii = at
                    sp.wait_ge(s["stage_free"], count(n - 1))
                    sp.dma_start(stage[tl % 2], ew_v[:, ds(ii * B + u, 1), tl, :].rearrange("p e o -> p (e o)")
                                 ).then_inc(s[f"stage_in{tl % 2}"], 16)
                at = ahead_tile(i, p, ROWS_AHEAD - 1, more)
                if at and at[2] == CT - 1 and more:
                    n, u, tl, ii = at
                    sp.wait_ge(s["xn_done"], count(n + 1))
                    sp.dma_start(x_in[u], x_v[u][:, ds((ii + 1) * CT, CT), :]).then_inc(s[f"x_in{u}"], 16)
                at = ahead_tile(i, p, 0, more)
                if at and at[2] % 2:
                    n, u, tl, ii = at
                    h = tl // 2
                    sp.wait_ge(s["kl_done"], count(n + 1))
                    for z, a in enumerate((k_hi, k_lo)):
                        sp.dma_start(k_v[z][u][:, :, ds(ii * CH + h * 2 * P, 2 * P)],
                                     a[:, :, h * 2 * P:(h + 1) * 2 * P]).then_inc(s[f"k_out{h}"], 16)
                    if tl == CT - 1:
                        sp.wait_ge(s["v_done"], count(n + 1))
                        sp.dma_start(v_v[u][:, :, ds(ii * (CT * V1), CT * V1)],
                                     v_st[u].rearrange("p h t f -> p h (t f)")).then_inc(s[f"v_out{u}"], 16)
                at = ahead_tile(i, p, ROWS_AHEAD, more)
                if at and at[2] % 2:
                    n, u, tl, ii = at
                    h = tl // 2
                    sp.wait_ge(s["xl_done"], count(n + 1))
                    sp.dma_start(xn_v[u][:, ds(ii * CT + h * 2, 2), :],
                                 x16[:, h * 2:h * 2 + 2].rearrange("p t z c -> p t (z c)")).then_inc(s[f"x_out{h}"], 16)
                at = ahead_tile(i, p, QUERIES_AHEAD, more)
                if at and at[2] % 2:
                    n, u, tl, ii = at
                    h = tl // 2
                    sp.wait_ge(s["ql_done"], count(n + 1))
                    for z, a in enumerate((q_hi, q_lo)):
                        sp.dma_start(q_v[z][u][:, :, ds(ii * CH + h * 2 * P, 2 * P)],
                                     a[:, :, h * 2 * P:(h + 1) * 2 * P]).then_inc(s[f"q_out{h}"], 16)

            run_tiles(sp, step)
            wait_stored(sp)

            def load_head(bh, u):
                for st, dram, order in ((q_st[u], q_dram, (0, 0, 1)), (k_st[u], k_dram, (0, 1, 0))):
                    for g, z in enumerate(order):
                        sp.dma_start(st[HD * g:HD * (g + 1), :], dram[z][ds(bh * HD, HD), :]).then_inc(s[f"ld{u}"], 16)
                sp.dma_start(v_sb[u], v_dram[ds(bh, 1), :, :, :].rearrange("o r j f -> (o r) j f")).then_inc(s[f"ld{u}"], 16)

            sp.wait_ge(s["stage_free"], count(NT))
            load_head(0, 0)
            load_head(1, 1)
            with sp.Fori(0, BH // 2 - 1) as it:
                for u in range(2):
                    sp.wait_ge(s["pv_done"], count(NU * (it * 2 + u + 1)))
                    load_head(it * 2 + u + 2, u)
            with sp.Fori(0, PT // 2) as i:
                for u in range(2):
                    sp.wait_ge(s["y_done"], count(i * 2 + u + 1))
                    sp.dma_start(y_dram[ds((i * 2 + u) * P, P), :], y_sb[u]).then_inc(s[f"y_st{u}"], 16)
            def residual(i, u):
                sp.dma_start(xc[u], xc_v[u][ds(i, 1), :, :].rearrange("t p d -> (t p) d")).then_inc(s[f"xc_in{u}"], 16)

            def result(i, u):
                sp.wait_ge(s["acc_done"], count(i * B + u + 1))
                sp.dma_start(out_v[u][ds(i, 1), :, :].rearrange("t p d -> (t p) d"), acc[u]).then_inc(s[f"out_done{u}"], 16)

            for u in range(B):
                residual(0, u)
            with sp.Fori(0, ST - 1) as i:
                for u in range(B):
                    result(i, u)
                    residual(i + 1, u)
            for u in range(B):
                result(ST - 1, u)
            for w in range(B):
                sp.wait_ge(s[f"out_done{w}"], count(16 * ST))

        @block.gpsimd
        def _(pool):
            g = nc.gpsimd
            start(pool, 1)
            link, _n = linker(pool, s["pool_link"])
            for t in (bdq, bdk, bdg, bdv, bdo):
                g.memset(t, 0.0)
            g.memset(ws_col[:], WS)
            g.memset(later[:], 0.0)
            g.memset(deny[:], 0.0)
            link(g.memset(eps[:], EPS))
            g.memset(ident[:], 0.0)
            g.memset(ident16[:], 0.0)
            g.memset(center, -1.0 / L)
            link(g.memset(tri[:], 0.0))
            g.sem_inc(s["zeroed"], 1)
            g.iota(iota[:], [[1, PT]], base=0, channel_multiplier=0, allow_small_or_imprecise_dtypes=True)
            g.memset(upper[:], 1.0)
            g.iota(token_id[:], [[P, NT]], base=0, channel_multiplier=1)
            link(g.memset(zero_ids[:], 0))
            g.affine_select(out=upper[:], in_=upper[:], compare_op=ALU.is_gt, fill=0.0, base=0,
                            pattern=[[1, P]], channel_multiplier=-1)
            for m in (ident, ident16):
                g.affine_select(out=m[:], in_=m[:], compare_op=ALU.not_equal, fill=1.0, base=0,
                                pattern=[[-1, P]], channel_multiplier=1)
            g.affine_select(out=center, in_=center, compare_op=ALU.not_equal, fill=1.0 - 1.0 / L, base=0,
                            pattern=[[-1, P]], channel_multiplier=1)
            g.affine_select(out=tri[:], in_=tri[:], compare_op=ALU.is_ge, fill=LOWEST, base=0,
                            pattern=[[-1, P]], channel_multiplier=1)
            g.affine_select(out=deny[:], in_=deny[:], compare_op=ALU.not_equal, fill=FAR, base=0,
                            pattern=[[-1, P]], channel_multiplier=1)
            g.affine_select(out=later[:], in_=later[:], compare_op=ALU.is_ge, fill=-FAR, base=0,
                            pattern=[[-P, 2], [1, 2 * P]], channel_multiplier=-1).then_inc(s["consts"], 1)
            base = _n[0]

            def step(i, p, more):
                at = ahead_tile(i, p, 0, more)
                if at:
                    n, u, tl, ii = at
                    lnk, cnt = linker(pool, s["pool_link"], n + base)
                    w = stage[tl % 2]
                    pool.wait_ge(s[f"stage_in{tl % 2}"], count((ii * (PER_IT // 2) + u * (CT // 2) + tl // 2 + 1) * 16))
                    hi = w_hi[:, ds(ii * B + u, 1), tl * E:(tl + 1) * E].rearrange("p e c -> p (e c)")
                    lo = w_lo[:, ds(ii * B + u, 1), tl * E:(tl + 1) * E].rearrange("p e c -> p (e c)")
                    g.tensor_tensor(hi, w, ws_col[:].to_broadcast([P, E]), ALU.mult)
                    lnk(g.tensor_tensor(w, w, ws_col[:].to_broadcast([P, E]), ALU.mult))
                    g.tensor_tensor(lo, w, hi, ALU.subtract).then_inc(s["stage_free"], 1)
                    assert cnt[0] == 1
                at = ahead_tile(i, p, QUERIES_AHEAD, more)
                if at:
                    n, u, tl, ii = at
                    pool.wait_ge(s["rs_done"], count(n + 1))
                    pool.wait_ge(s["tr2_ps"], count(n - 1))
                    g.tensor_tensor(xr[tl % 2].rearrange("p (h d) -> p h d", h=H), xn[:, tl, :].rearrange("p (h d) -> p h d", h=H),
                                    rs[tl % 2][:].unsqueeze(2).to_broadcast([P, H, HD]), ALU.mult).then_inc(s["xr_done"], 1)

            assert CT == KB
            run_tiles(pool, step)
            pool.dma_start(id_dram.rearrange("(p t) o -> p (t o)", p=P), zero_ids[:]).then_inc(s["id_zero"], 16)
            pool.wait_ge(s["id_zero"], 16)
            pool.wait_ge(s["placed"], count(1))
            with pool.Fori(0, NT) as i:
                g.tensor_copy(cur[:, 0:TOP], place_at[:, :, ds(i, 1)].rearrange("p k o -> p (k o)"))
                g.tensor_copy(cur_id[:, 0:1], token_id[:, ds(i, 1)])
                g.drain()
                for k in range(TOP):
                    g.indirect_dma_start(out=id_dram, out_offset=bass.IndirectOffsetOnAxis(ap=cur[:, k:k + 1], axis=0),
                                         in_=cur_id[:, 0:1], in_offset=None).then_inc(s["id_done"], 16)
                pool.wait_ge(s["id_done"], (i + 1) * (16 * TOP))
            pool.wait_ge(s["id_done"], 16 * TOP * NT)
            pool.dma_start(ids[:], id_dram.rearrange("(p t) o -> p (t o)", p=P)).then_inc(s["ids_in"], 16)
            pool.wait_ge(s["ids_in"], 16)

            def gathers(i, first):
                for q in range(AHEAD_G):
                    n = i * AHEAD_G + q
                    if first and q == 1:
                        pool.wait_ge(s["norm_done"], count(NC * BH))
                    pool.wait_ge(s["gt_ps"], count(n - AHEAD_G + 1))
                    g.tensor_copy(cur_id[:, q:q + 1], ids[:, ds(n, 1)]).then_inc(s["cur_done"], 1)
                    pool.wait_ge(s["cur_done"], count(n + 1))
                    pool.sem_inc(s["gather_at"], 1)
                    g.indirect_dma_start(out=x_g[q], out_offset=None, in_=xn_dram,
                                         in_offset=bass.IndirectOffsetOnAxis(ap=cur_id[:, q:q + 1], axis=0)
                                         ).then_inc(s[f"xg_in{q}"], 16)

            gathers(0, True)
            with pool.Fori(1, PT // AHEAD_G) as i:
                gathers(i, False)
            for u in range(2):
                pool.wait_ge(s[f"y_st{u}"], count(16 * PT // 2))
            with pool.Fori(0, ST) as i:
                for u in range(B):
                    n = i * B + u
                    pool.wait_ge(s["acc_done"], count(n - 1))
                    g.tensor_copy(cur[:, TOP * u:TOP * (u + 1)],
                                  place[:, :, ds(i + u * ST, 1)].rearrange("p k o -> p (k o)")).then_inc(s["cur_done"], 1)
                    pool.wait_ge(s["cur_done"], count(PT + n + 1))
                    pool.sem_inc(s["gather_at"], 1)
                    for k in range(TOP):
                        g.indirect_dma_start(out=y_g[u][k], out_offset=None, in_=y_dram,
                                             in_offset=bass.IndirectOffsetOnAxis(ap=cur[:, TOP * u + k:TOP * u + k + 1], axis=0)
                                             ).then_inc(s[f"yg_in{u}"], 16)

        @block.scalar
        def _(act):
            a = nc.scalar
            start(act, 2)
            with nc.allow_non_contiguous_dma(reason="small per-head vectors, once"):
                act.dma_start(g_t, ln_g.rearrange("h l -> l h")).then_inc(s["g_in"], 16)
                act.dma_start(b_t, ln_b.rearrange("h l -> l h")).then_inc(s["g_in"], 16)
            act.dma_start(wo_raw, Wo.rearrange("(n p) c -> p n c", p=P)).then_inc(s["wo_in"], 16)
            act.dma_start(gw_raw[:], gate_w.rearrange("(k p) e -> p k e", p=P)).then_inc(s["gate_in"], 16)
            act.dma_start(gb_bc[:], gate_b.partition_broadcast(P)).then_inc(s["gate_in"], 16)
            act.dma_start(bo_bc[:], bo.partition_broadcast(P)).then_inc(s["bias_in"], 16)
            act.dma_start(eb_bc[:], expert_b.partition_broadcast(P)).then_inc(s["bias_in"], 16)
            act.wait_ge(s["bias_in"], count(32))
            a.activation(eb_bc[:].rearrange("p e c -> p (e c)"), eb_bc[:].rearrange("p e c -> p (e c)"), ACT.Copy,
                         scale=1.0 / TOP).then_inc(s["eb_done"], 1)
            for k in range(KB):
                act.wait_ge(s["wot_ps"], count(k + 1))
                a.activation(wo_t[:, k, :], PS[:, 6 + k % 2, :], ACT.Copy).then_inc(s["wot_done"], 1)
            for k in range(KB):
                act.wait_ge(s["comb_ps"], count(k + 1))
                a.activation(comb_hl[:, 0, k, :], PS[:, 4 + k, :], ACT.Copy, scale=WS).then_inc(s["comb_hi"], 1)
            def spread(chunk):
                act.wait_ge(s["mv_done"], count(chunk + 1))
                a.activation(sd4[:], mv[:, :, 1], ACT.Sqrt, bias=eps[:]).then_inc(s["sd4_done"], 1)

            def step(i, p, more):
                at = ahead_tile(i, p, 0, more)
                if at:
                    n, u, tl, ii = at
                    act.wait_ge(s["tr2_ps"], count(n + 1))
                    act.wait_ge(s["vv_ps"], count(n - 1))
                    a.activation(xrT[tl % 2].rearrange("p k c -> p (k c)"), PS[:, 4, :], ACT.Copy).then_inc(s["xrt_done"], 1)
                at = ahead_tile(i, p, ROWS_AHEAD, more)
                if at:
                    n, u, tl, ii = at
                    act.wait_ge(s["xn_done"], count(n + 1))
                    act.wait_ge(s["tp_ps"], count(n - CT + 1))
                    act.wait_ge(s[f"x_out{tl // 2}"], count((ii * B + u) * 16))
                    a.activation(x16[:, tl, 0], xn[:, tl], ACT.Copy).then_inc(s["xh_done"], 1)
                at = ahead_tile(i, p, QUERIES_AHEAD, more)
                if at:
                    n, u, tl, ii = at
                    act.wait_ge(s["q_ps"], count(n + 1))
                    act.wait_ge(s[f"q_out{tl // 2}"], count((ii * B + u) * 32))
                    a.activation(q_hi[:, :, tl * P:(tl + 1) * P], PS[:, 1, :].rearrange("p (k c) -> p k c", k=KB), ACT.Copy,
                                 scale=1.0 / WS).then_inc(s["qh_done"], 1)
                at = ahead_tile(i, p, 0, more)
                if at:
                    n, u, tl, ii = at
                    act.wait_ge(s["k_ps"], count(n + 1))
                    act.wait_ge(s[f"k_out{tl // 2}"], count((ii * B + u) * 32))
                    for k in range(KB):
                        last = a.activation(k_hi[:, k, tl * P:(tl + 1) * P], PS[:, 5, k * P:(k + 1) * P], ACT.Identity,
                                            bias=bk[:, k:k + 1])
                    last.then_inc(s["kh_done"], 1)
                    act.wait_ge(s["vv_ps"], count(n + 1))
                    act.wait_ge(s[f"v_out{u}"], count(ii * 16))
                    a.activation(v_st[u][:, :, tl, 0:HD], PS[:, 6, :].rearrange("p (h d) -> p h d", h=H),
                                 ACT.Copy).then_inc(s["v_done"], 1)
                at = ahead_tile(i, p, TURN_AHEAD, more)
                if at:
                    n, u, tl, ii = at
                    act.wait_ge(s["tp_ps"], count(n + 1))
                    act.wait_ge(s["g_ps"], count(n - 1))
                    a.activation(xT[tl % 2].rearrange("p z k c -> p (z k c)"), PS[:, 2:4, :].rearrange("p z c -> p (z c)"),
                                 ACT.Copy).then_inc(s["xt_done"], 1)
                at = ahead_tile(i, p, QUERIES_AHEAD, more)
                if at:
                    n, u, tl, ii = at
                    act.wait_ge(s["var_done"], count(n + 1))
                    act.wait_ge(s["rs_done"], count(n - 1))
                    a.activation(sd[tl % 2][:], var[tl % 2][:], ACT.Sqrt, bias=eps[:], scale=1.0 / WS).then_inc(s["sd_done"], 1)
                at = ahead_tile(i, p, ROWS_AHEAD + 1, more)
                if at and at[2] == 0:
                    spread(at[3] * B + at[1])

            spread(0)
            run_tiles(act, step)
            def max_row(sh, w, c, bank):
                act.wait_ge(s["m_ps"], count(sh * NC + c + 1))
                a.activation(q_st[w][3 * HD:3 * HD + 1, c * CH:(c + 1) * CH], PS[3 * HD:3 * HD + 1, bank, :],
                             ACT.Copy).then_inc(s["m_done"], 1)

            def heads(it, more, span):
                for kk in span:
                    if kk < 2 * NU or more:
                        c, j, (wa, wb), off, _m = UNITS[kk % NU]
                        act.wait_ge(s["s2_ps"], count(it * (2 * NU) + kk + 1))
                        act.wait_ge(s["pv_done"], count(it * (2 * NU) + kk - 3))
                        z = PS[:, 2 + 2 * (kk % 2):4 + 2 * (kk % 2), :].rearrange("p a s -> p (a s)")
                        a.activation(probs[kk % 4][:, 0:off + wb], z[:, 0:off + wb], ACT.Exp,
                                     scale=SCALE).then_inc(s["exp_done"], 1)
                        u, k = divmod(kk, NU)
                        for ahead, cc in slot_max_rows(k):
                            if u + ahead < 2 or more:
                                max_row(it * 2 + u + ahead, (u + ahead) % 2, cc, free_bank(kk))
                    pk = kk - PV_LAG
                    if 0 <= pk < 2 * NU and pk % NU in LAST:
                        q = (pk // NU) * NC + LAST[pk % NU]
                        act.wait_ge(s["pv_done"], count(it * (2 * NU) + pk + 1))
                        act.wait_ge(s["tr_ps"], count(it * (2 * NC) + q - 1))
                        a.activation(ot[q % 2][0:2 * HD + V1, :], PS[0:2 * HD + V1, 6 + q % 2, :], ACT.Copy).then_inc(s["ot_done"], 1)

            for c in range(NC - 1):
                max_row(0, 0, c, 7)
            heads(0, True, LEAD)
            with act.Fori(0, BH // 2 - 1) as it:
                heads(it, True, SPAN)
            heads(BH // 2 - 1, False, SPAN)
            def turned(n, u):
                act.wait_ge(s["gt_ps"], count(n + 1))
                act.wait_ge(s["z_ps"], count(n - 1))
                a.activation(xg_T[u].rearrange("p z k c -> p (z k c)"),
                             PS[:, 4 + 2 * u:6 + 2 * u, :].rearrange("p z c -> p (z c)"), ACT.Copy).then_inc(s["gT_done"], 1)

            with act.Fori(0, PT // 2) as i:
                for u in range(2):
                    turned(i * 2 + u, u)

            def first_piece(i, u):
                n = i * B + u
                act.wait_ge(s["otp_ps"], count(n - 1))
                a.activation(o16[u][:, 0].rearrange("p (h d) -> p h d", h=H),
                             attn[:, ds(i, 1), u * H:(u + 1) * H, :].rearrange("p t h d -> p (t h) d"),
                             ACT.Copy).then_inc(s["o_hi_done"], 1)

            def turned_heads(n, u):
                act.wait_ge(s["otp_ps"], count(n + 1))
                act.wait_ge(s["proj_ps"], count(n - 1))
                a.activation(oT[u].rearrange("p z k c -> p (z k c)"),
                             PS[:, 4 + 2 * u:6 + 2 * u, :].rearrange("p z c -> p (z c)"), ACT.Copy).then_inc(s["oT_done"], 1)

            for u in range(B):
                first_piece(0, u)
            with act.Fori(0, ST - 1) as i:
                for u in range(B):
                    turned_heads(i * B + u, u)
                    first_piece(i + 1, u)
            for u in range(B):
                turned_heads((ST - 1) * B + u, u)

        @block.vector
        def _(dve):
            v = nc.vector
            start(dve, 3)
            link, n0 = linker(dve, s["dve0"])
            def means(u, ii, tiles):
                if 0 in tiles:
                    dve.wait_ge(s[f"x_in{u}"], count((ii + 1) * 16))
                for t in tiles:
                    v.bn_stats(stats[:, t, :], x_in[u][:, t, :])
                if CT - 1 not in tiles:
                    return
                v.drain()
                for t in range(CT):
                    last = v.bn_aggr(mv[:, t, :], stats[:, t, :])
                last.then_inc(s["mv_done"], 1)

            dve.wait_ge(s["g_in"], count(32))
            dve.wait_ge(s["w_in"], count(48))

            def per_head(t):
                return t.rearrange("p (h d) -> p h d", h=H)
            v.memset(ones, 1.0)
            for w, vec, r in ((wuk, g_t, gwuk), (wuv, g_t, gwuv), (wuv, b_t, bwuv)):
                last = v.tensor_tensor(per_head(r), per_head(w), vec.unsqueeze(2).to_broadcast([P, H, HD]), ALU.mult)
            last.then_inc(s["gw_done"], 1)
            dve.wait_ge(s["wc_ps"], count(1))
            v.tensor_copy(wc, PS[:, 0, :]).then_inc(s["wc_done"], 1)
            dve.wait_ge(s["gate_in"], count(32))
            link(v.tensor_scalar(gw_raw[:], gw_raw[:], WS, None, ALU.mult))
            link(v.tensor_copy(gw_hl[:, :, 0], gw_raw[:]))
            v.tensor_tensor(gw_hl[:, :, 1], gw_raw[:], gw_hl[:, :, 0], ALU.subtract).then_inc(s["gates_done"], 1)
            means(0, 0, range(CT))
            dve.wait_ge(s["fold_ps"], count(1))
            for b, bd, scale in ((2, bdg, WS / L), (1, bdk, 1.0), (3, bdv, 1.0)):
                for j in range(HK):
                    r = slice(HD * j, HD * (j + 1))
                    v.tensor_scalar(bd[r, :, r], PS[r, b, :].rearrange("p (k c) -> p k c", k=KB)[:, :, r], scale, None, ALU.mult)
            for j in range(HK):
                r = slice(HD * j, HD * (j + 1))
                v.tensor_copy(bk[r, :], PS[r, 4, 0:H].rearrange("p (k j) -> p k j", k=KB)[:, :, j])
            v.tensor_copy(bv_bc[:], PS[:, 5, :]).then_inc(s["fold_done"], 1)
            dve.wait_ge(s["wqo_in"], count(16 * 2 * HK))
            dve.wait_ge(s["fold_done"], count(1))
            link(v.tensor_tensor(gwuk, bdo.rearrange("p k c -> p (k c)"), bv_bc[:], ALU.mult))
            v.reduce_sum(bo_c, gwuk.rearrange("p (k c) -> p k c", k=KB), AX).then_inc(s["boc_done"], 1)
            link(v.tensor_scalar(bdq, bdq, WS, None, ALU.mult))
            v.tensor_copy(bdg_hl[:, 0], bdg)
            link(v.tensor_copy(bdq_hl[:, 0], bdq))
            v.tensor_tensor(bdg_hl[:, 1], bdg, bdg_hl[:, 0], ALU.subtract)
            v.tensor_tensor(bdq_hl[:, 1], bdq, bdq_hl[:, 0], ALU.subtract).then_inc(s["bd_done"], 1)
            dve.wait_ge(s["bias_in"], count(32))
            link(v.tensor_scalar(bo_bc[:], bo_bc[:], 1.0 / TOP, None, ALU.mult))
            dve.wait_ge(s["bob_ps"], count(1))
            v.scalar_tensor_tensor(out=bo_bc[:], in0=PS[:, 2, :], scalar=1.0 / TOP, in1=bo_bc[:],
                                   op0=ALU.mult, op1=ALU.add).then_inc(s["bob_done"], 1)
            for k in range(KB):
                dve.wait_ge(s["comb_hi"], count(k + 1))
                v.scalar_tensor_tensor(out=comb_hl[:, 1, k, :], in0=PS[:, 4 + k, :], scalar=WS, in1=comb_hl[:, 0, k, :],
                                       op0=ALU.mult, op1=ALU.subtract).then_inc(s["comb_done"], 1)
            dve.wait_ge(s["consts"], count(1))
            for u in range(2):
                last = v.memset(v_st[u][:, :, :, HD:V1], 1.0)
            link(last)

            def step(i, p, more):
                at = ahead_tile(i, p, ROWS_AHEAD, more)
                if at:
                    n, u, tl, ii = at
                    chunk = ii * B + u
                    if tl == 0:
                        lnk, cnt = linker(dve, s["dve_rows"], chunk)
                        dve.wait_ge(s["sd4_done"], count(chunk + 1))
                        lnk(v.reciprocal(rs4[:], sd4[:]))
                    dve.wait_ge(s["xr_done"], count(n - CT + 1))
                    v.tensor_scalar(xn[:, tl, :], x_in[u][:, tl, :], mv[:, tl, 0:1], rs4[:, tl:tl + 1],
                                    ALU.subtract, ALU.mult).then_inc(s["xn_done"], 1)
                at = ahead_tile(i, p, QUERIES_AHEAD, more)
                if at:
                    n, u, tl, ii = at
                    dve.wait_ge(s["y_ps"], count(n + 1))
                    dve.wait_ge(s["sd_done"], count(n - 1))
                    v.tensor_tensor(prod, PS[:, 0, :], xn[:, tl, :], ALU.mult).then_inc(s["prod_done"], 1)
                at = ahead_tile(i, p, ROWS_AHEAD, more)
                if at:
                    n, u, tl, ii = at
                    dve.wait_ge(s["xh_done"], count(n + 1))
                    v.tensor_tensor(x16[:, tl, 1], xn[:, tl], x16[:, tl, 0], ALU.subtract).then_inc(s["xl_done"], 1)
                at = ahead_tile(i, p, QUERIES_AHEAD, more)
                if at:
                    n, u, tl, ii = at
                    dve.wait_ge(s["prod_done"], count(n + 1))
                    v.reduce_sum(var[tl % 2][:], prod.rearrange("p (h d) -> p h d", h=H), AX).then_inc(s["var_done"], 1)
                    dve.wait_ge(s["qh_done"], count(n + 1))
                    v.scalar_tensor_tensor(out=q_lo[:, :, tl * P:(tl + 1) * P], in0=PS[:, 1, :].rearrange("p (k c) -> p k c", k=KB),
                                           scalar=1.0 / WS, in1=q_hi[:, :, tl * P:(tl + 1) * P],
                                           op0=ALU.mult, op1=ALU.subtract).then_inc(s["ql_done"], 1)
                at = ahead_tile(i, p, 0, more)
                if at:
                    n, u, tl, ii = at
                    dve.wait_ge(s["kh_done"], count(n + 1))
                    for k in range(KB):
                        c = slice(tl * P, (tl + 1) * P)
                        last = v.scalar_tensor_tensor(out=k_lo[:, k, c], in0=PS[:, 5, k * P:(k + 1) * P], scalar=bk[:, k:k + 1],
                                                      in1=k_hi[:, k, c], op0=ALU.add, op1=ALU.subtract)
                    last.then_inc(s["kl_done"], 1)
                at = ahead_tile(i, p, QUERIES_AHEAD, more)
                if at:
                    n, u, tl, ii = at
                    dve.wait_ge(s["sd_done"], count(n + 1))
                    dve.wait_ge(s["xr_done"], count(n - 1))
                    v.reciprocal(rs[tl % 2][:], sd[tl % 2][:]).then_inc(s["rs_done"], 1)
                if at and at[2] == CT - 1:
                    lnk, cnt = linker(dve, s["dve_gates"], (ii * B + u) * 2)
                    dve.wait_ge(s["g_ps"], count(n + 1))
                    G = PS[:, 7, 0:CT * 2 * NE].rearrange("p (t z e) -> p t z e", t=CT, z=2)
                    lnk(v.scalar_tensor_tensor(out=lg[:], in0=G[:, :, 0, :], scalar=1.0 / WS,
                                               in1=gb_bc[:].unsqueeze(1).to_broadcast([P, CT, NE]), op0=ALU.mult, op1=ALU.add))
                    v.scalar_tensor_tensor(out=lg[:], in0=G[:, :, 1, :], scalar=1.0 / WS, in1=lg[:],
                                           op0=ALU.mult, op1=ALU.add).then_inc(s["lg_done"], 1)
                    v.drain()
                    for t in range(CT):
                        v.max(top8[:, t, :], lg[:, t, :])
                    v.drain()
                    for t in range(CT):
                        v.max_index(idx8[:, t, :], top8[:, t, :], lg[:, t, :])
                    v.drain()
                    lnk(v.tensor_copy(idxf[:], idx8[:]))
                    for k in range(TOP):
                        v.tensor_tensor(chosen[:, k, ds(ii * CT + u * ST, CT), :],
                                        iota[:, 0:NE].unsqueeze(1).to_broadcast([P, CT, NE]),
                                        idxf[:, :, k:k + 1].to_broadcast([P, CT, NE]), ALU.is_equal)
                    assert cnt[0] == 2
                at = ahead_tile(i, p, ROWS_AHEAD + 3, more)
                if at and at[2] < CT - 1:
                    means(at[1], at[3], (at[2],) if at[2] < CT - 2 else (CT - 2, CT - 1))

            run_tiles(dve, step)
            lnk, cnt = linker(dve, s["dveR"])
            v.memset(ones16, 1.0)
            v.memset(r_ones, 1.0)
            v.memset(r_exp, 0.0)
            v.tensor_tensor(r_m16.rearrange("p (g e) -> p g e", e=NE), chosen[:, 0], chosen[:, 1], ALU.add).then_inc(s["counted"], 1)
            dve.wait_ge(s["cnt_ps"], count(1))
            ge, eg = "p (g e) -> p g e", "p (e g) -> p e g"
            v.tensor_copy(r_in, PS[:, 7, 0:NT * NE])
            v.tensor_copy(r_tot.rearrange(eg, e=NE), PS[:, 7, NT * NE:2 * NT * NE].rearrange("p (g e) -> p e g", e=NE)).then_inc(s["cnt_done"], 1)
            dve.wait_ge(s["cnt_done"], count(1))
            for e in range(NE):
                c = slice(e * NT, (e + 1) * NT)
                last = v.tensor_tensor_scan(r_incl[:, c], r_ones, r_tot[:, c], 0.0, ALU.mult, ALU.add)
            lnk(last)
            lnk(v.tensor_scalar(r_n, r_incl.rearrange(eg, e=NE)[:, :, NT - 1], float(P - 1), None, ALU.add))
            lnk(v.tensor_copy(r_int[:, 0:NE], r_n))
            lnk(v.tensor_scalar(r_int2[:, 0:NE], r_int[:, 0:NE], 7, None, ALU.arith_shift_right))
            lnk(v.tensor_copy(r_tiles, r_int2[:, 0:NE]))
            lnk(v.tensor_tensor_scan(r_cum, r_ones[:, 0:NE], r_tiles, 0.0, ALU.mult, ALU.add))
            lnk(v.tensor_tensor(r_base, r_cum, r_tiles, ALU.subtract))
            lnk(v.tensor_scalar(r_base, r_base, float(P), None, ALU.mult))
            lnk(v.tensor_tensor(r_incl, r_incl, r_tot, ALU.subtract))
            lnk(v.tensor_tensor(r_incl.rearrange(eg, e=NE), r_incl.rearrange(eg, e=NE),
                                r_base.unsqueeze(2).to_broadcast([P, NE, NT]), ALU.add))
            lnk(v.tensor_tensor(r_slot.rearrange(ge, e=NE), r_in.rearrange(ge, e=NE),
                                r_incl.rearrange("p (e g) -> p g e", e=NE), ALU.add))
            for k in range(TOP):
                lnk(v.tensor_tensor(r_tmp.rearrange(ge, e=NE), chosen[:, k], r_slot.rearrange(ge, e=NE), ALU.mult))
                lnk(v.reduce_sum(r_f[:, k * NT:(k + 1) * NT], r_tmp.rearrange(ge, e=NE), AX))
            v.tensor_copy(place[:].rearrange("p k g -> p (k g)"), r_f)
            lnk(v.tensor_copy(r_int, r_f))
            lnk(v.tensor_scalar(r_int2, r_int, P - 1, None, ALU.bitwise_and))
            lnk(v.tensor_copy(r_tmp[:, 0:NT * TOP], r_int2))
            lnk(v.tensor_scalar(r_int2, r_int, 7, None, ALU.arith_shift_right))
            lnk(v.tensor_copy(r_f, r_int2))
            v.scalar_tensor_tensor(out=place_at[:].rearrange("p k g -> p (k g)"), in0=r_tmp[:, 0:NT * TOP], scalar=float(PT),
                                   in1=r_f, op0=ALU.mult, op1=ALU.add)
            for e in range(NE):
                lnk(v.scalar_tensor_tensor(out=r_exp, in0=iota[:], scalar=r_cum[:, e:e + 1], in1=r_exp,
                                           op0=ALU.is_ge, op1=ALU.add))
            v.tensor_scalar(expert_of[:], r_exp, float(NE - 1), None, ALU.min).then_inc(s["placed"], 1)
            dve.wait_ge(s["stage_free"], count(NT))
            wait_stored(dve)
            for w in range(2):
                v.memset(k_st[w][3 * HD:3 * HD + 1, :].bitcast(f32), float(np.full(2, -MS, np.float16).view(np.float32)[0]))
            v.memset(pm[:], LOWEST)
            v.memset(PS[:, 6:8, :], 0.0).then_inc(s["b_zero"], 1)
            dve.wait_ge(s["b_zero"], count(1))
            def piece(sh, n):
                i, p, w = PIECES[n]
                c, r = divmod(i, CT)
                seq = sh * NP_ + n
                dve.wait_ge(s["s1_ps"], count(seq + 1))
                bank = n % 2
                if p < i // CT:
                    ins = v.reduce_max(pm[:, c, r, p:p + 1], PS[:, bank, 0:w], AX)
                else:
                    v.reduce_max(pm[:, c, r, p:p + 1], PS[:, bank, 0:w - P + 1], AX)
                    ins = v.tensor_tensor_reduce(out=junk[:, r, :], in0=PS[:, bank, w - P:w], in1=tri[:], scale=1.0,
                                                 scalar=LOWEST, op0=ALU.add, op1=ALU.max,
                                                 accum_out=pm[:, c, r, PMS - 1:PMS])
                ins.then_inc(s["s1_done"], 1)
                if n in CHUNK_END:
                    dve.wait_ge(s["s1_done"], count(seq + 1))
                    v.reduce_max(mx[:, c, :], pm[:, c, :, :], AX).then_inc(s["mx_done"], 1)
                    dve.wait_ge(s["mx_done"], count((sh * NC + c) * 2 + 1))
                    v.tensor_scalar(mx16[:, c, :], mx[:, c, :], 1.0 / MS, None, ALU.mult).then_inc(s["mx_done"], 1)

            def norm(it, q):
                lnk, cnt = linker(dve, s["dveB"], (it * (2 * NC) + q) * 3)
                dve.wait_ge(s["tr_ps"], count(it * (2 * NC) + q + 1))
                T = PS[:, 6 + q % 2, 0:CT * (2 * HD + V1)].rearrange("p (t f) -> p t f", t=CT)
                dve.wait_ge(s["norm_done"], count(it * (2 * NC) + q))
                lnk(v.tensor_copy(half_b[:], T[:, :, 2 * HD:2 * HD + V1]))
                lnk(v.tensor_tensor(whole[:], T[:, :, 0:V1], half_b[:], ALU.add))
                lnk(v.reciprocal(rden[:], whole[:, :, HD:V1]))
                u, c = divmod(q, NC)
                v.tensor_tensor(attn[:, CT * c:CT * (c + 1), ds(it * 2 + u, 1), :].rearrange("p t o d -> p t (o d)"),
                                whole[:, :, 0:HD], rden[:].to_broadcast([P, CT, HD]), ALU.mult).then_inc(s["norm_done"], 1)

            def heads(it, more, span):
                for kk in span:
                    u, k = divmod(kk, NU)
                    if kk < 2 * NU or more:
                        for ahead, n in slot_pieces(k):
                            if u + ahead < 2 or more:
                                piece(it * 2 + u + ahead, n)
                    pk = kk - PV_LAG - 1
                    if pk >= 0 and pk % NU in LAST:
                        norm(it, (pk // NU) * NC + LAST[pk % NU])

            for n in range(EARLY):
                piece(0, n)
            heads(0, True, LEAD)
            with dve.Fori(0, BH // 2 - 1) as it:
                heads(it, True, SPAN)
            heads(BH // 2 - 1, False, SPAN)
            dve.wait_ge(s["eb_done"], count(1))
            with dve.Fori(0, PT // 2) as i:
                for u in range(2):
                    n = i * 2 + u
                    e = dve.value_load(expert_of[0:1, ds(n, 1)], min_val=0, max_val=NE - 1)
                    dve.wait_ge(s["z_ps"], count(n + 1))
                    dve.wait_ge(s[f"y_st{u}"], count(i * 16))
                    v.scalar_tensor_tensor(out=y_sb[u], in0=PS[:, u, :], scalar=1.0 / (WS * TOP),
                                           in1=eb_bc[:, ds(e, 1), :].rearrange("p e c -> p (e c)"),
                                           op0=ALU.mult, op1=ALU.add).then_inc(s["half_done"], 1)
                    dve.wait_ge(s["half_done"], count(n + 1))
                    v.scalar_tensor_tensor(out=y_sb[u], in0=y_sb[u], scalar=0.0, in1=bo_bc[:],
                                           op0=ALU.max, op1=ALU.add).then_inc(s["y_done"], 1)

            def second_piece(i, u):
                n = i * B + u
                dve.wait_ge(s["o_hi_done"], count(n + 1))
                v.tensor_tensor(o16[u][:, 1].rearrange("p (h d) -> p h d", h=H),
                                attn[:, ds(i, 1), u * H:(u + 1) * H, :].rearrange("p t h d -> p (t h) d"),
                                o16[u][:, 0].rearrange("p (h d) -> p h d", h=H), ALU.subtract).then_inc(s["o_lo_done"], 1)

            def sums(i, u):
                n = i * B + u
                lnk, cnt = linker(dve, s["dveE"], n * 2)
                dve.wait_ge(s[f"out_done{u}"], count(i * 16))
                dve.wait_ge(s[f"xc_in{u}"], count((i + 1) * 16))
                dve.wait_ge(s["proj_ps"], count(n + 1))
                lnk(v.scalar_tensor_tensor(out=acc[u], in0=PS[:, u, :], scalar=1.0 / WS, in1=xc[u], op0=ALU.mult, op1=ALU.add))
                dve.wait_ge(s[f"yg_in{u}"], (i + 1) * (16 * TOP))
                lnk(v.tensor_tensor(acc[u], acc[u], y_g[u][0], ALU.add))
                v.tensor_tensor(acc[u], acc[u], y_g[u][1], ALU.add).then_inc(s["acc_done"], 1)

            for u in range(B):
                second_piece(0, u)
            with dve.Fori(0, ST - 1) as i:
                for u in range(B):
                    second_piece(i + 1, u)
                    sums(i, u)
            for u in range(B):
                sums(ST - 1, u)

        @block.tensor
        def _(pe):
            t = nc.tensor
            start(pe, 4)
            pe.wait_ge(s["consts"], count(1))
            pe.wait_ge(s["w_in"], count(48))
            t.matmul(PS[:, 0, :], center, wdkv, start=True, stop=True).then_inc(s["wc_ps"], 1)
            pe.wait_ge(s["gw_done"], count(1))
            t.matmul(PS[:, 5, :], ones, bwuv, start=True, stop=True)
            for k in range(KB):
                c = slice(P * k, P * (k + 1))
                t.matmul(PS[:, 4, HK * k:HK * (k + 1)], wuk[:, c], b_t[:, HK * k:HK * (k + 1)], start=True, stop=True)
            pe.wait_ge(s["wc_done"], count(1))
            for k in range(KB):
                c = slice(P * k, P * (k + 1))
                t.matmul(PS[:, 2, c], wc[:, c], wc[:, c], start=True, stop=True)
                t.matmul(PS[:, 1, c], wc[:, c], gwuk[:, c], start=True, stop=True)
                last = t.matmul(PS[:, 3, c], wc[:, c], gwuv[:, c], start=True, stop=True)
            last.then_inc(s["fold_ps"], 1)
            pe.wait_ge(s["wo_in"], count(16))
            for k in range(KB):
                for n in range(4):
                    last = t.transpose(PS[:, 6 + k % 2, n * P:(n + 1) * P], wo_raw[:, n, k * P:(k + 1) * P], ident[:])
                last.then_inc(s["wot_ps"], 1)
                if k % 2:
                    pe.wait_ge(s["wot_done"], count(k + 1))
            pe.wait_ge(s["fold_done"], count(1))
            pe.wait_ge(s["wqo_in"], count(16 * 2 * HK))
            for k in range(KB):
                t.matmul(PS[:, 4 + k, :], bdo[:, k, :], wo_t[:, k, :], start=True, stop=True).then_inc(s["comb_ps"], 1)
            pe.wait_ge(s["boc_done"], count(1))
            for k in range(KB):
                last = t.matmul(PS[:, 2, :], bo_c[:, k:k + 1].to_broadcast([P, P]), wo_t[:, k, :], start=k == 0, stop=k == KB - 1)
            last.then_inc(s["bob_ps"], 1)
            pe.wait_ge(s["bob_done"], count(1))
            pe.wait_ge(s["comb_done"], count(KB))
            pe.wait_ge(s["gates_done"], count(1))
            pe.wait_ge(s["bd_done"], count(1))

            def step(i, p, more):
                at = ahead_tile(i, p, 0, more)
                if at:
                    n, u, tl, ii = at
                    pe.wait_ge(s["xr_done"], count(n + 1))
                    pe.wait_ge(s["xrt_done"], count(n))
                    for k in range(KB):
                        last = t.transpose(PS[:, 4, k * P:(k + 1) * P], xr[tl % 2][:, k * P:(k + 1) * P], ident[:])
                    last.then_inc(s["tr2_ps"], 1)
                at = ahead_tile(i, p, QUERIES_AHEAD, more)
                if at:
                    n, u, tl, ii = at
                    pe.wait_ge(s["xt_done"], count(n + 1))
                    pe.wait_ge(s["prod_done"], count(n))
                    x_ = xT[tl % 2]
                    pairs = ((0, 0), (1, 0), (0, 1))
                    for k in range(KB):
                        for q, (z, w) in enumerate(pairs):
                            last = t.matmul(PS[:, 0, k * P:(k + 1) * P], x_[:, z, k, :], bdg_hl[:, w, k, :],
                                            start=q == 0, stop=q == len(pairs) - 1)
                    last.then_inc(s["y_ps"], 1)
                    pe.wait_ge(s["ql_done"], count(n))
                    for k in range(KB):
                        for q, (z, w) in enumerate(pairs):
                            last = t.matmul(PS[:, 1, k * P:(k + 1) * P], bdq_hl[:, w, k, :], x_[:, z, k, :],
                                            start=q == 0, stop=q == len(pairs) - 1)
                    last.then_inc(s["q_ps"], 1)
                    if tl == 0:
                        pe.wait_ge(s["lg_done"], count(ii * B + u))
                    for k in range(KB):
                        for z in range(2):
                            last = t.matmul(PS[:, 7, tl * 2 * NE:(tl + 1) * 2 * NE], x_[:, z, k, :],
                                            gw_hl[:, k].rearrange("p y e -> p (y e)"),
                                            start=(k, z) == (0, 0), stop=(k, z) == (KB - 1, 1))
                    last.then_inc(s["g_ps"], 1)
                at = ahead_tile(i, p, 0, more)
                if at:
                    n, u, tl, ii = at
                    pe.wait_ge(s["xrt_done"], count(n + 1))
                    pe.wait_ge(s["kl_done"], count(n))
                    for k in range(KB):
                        last = t.matmul(PS[:, 5, k * P:(k + 1) * P], bdk[:, k, :], xrT[tl % 2][:, k, :], start=True, stop=True)
                    last.then_inc(s["k_ps"], 1)
                    pe.wait_ge(s["v_done"], count(n))
                    for k in range(KB):
                        last = t.matmul(PS[:, 6, k * P:(k + 1) * P], xrT[tl % 2][:, k, :], bdv[:, k, :], start=True, stop=True)
                    last.then_inc(s["vv_ps"], 1)
                at = ahead_tile(i, p, TURN_AHEAD, more)
                if at:
                    n, u, tl, ii = at
                    pe.wait_ge(s["xl_done"], count(n + 1))
                    pe.wait_ge(s["xt_done"], count(n))
                    for z in range(2):
                        for k in range(KB):
                            last = t.matmul(PS[:, 2 + z, k * P:(k + 1) * P], x16[:, tl, z, k * P:(k + 1) * P], ident16[:],
                                            start=True, stop=True)
                    last.then_inc(s["tp_ps"], 1)

            run_tiles(pe, step)
            pe.wait_ge(s["counted"], count(1))
            t.matmul(PS[:, 7, 0:NT * NE], upper[:], r_m16, start=True, stop=True)
            t.matmul(PS[:, 7, NT * NE:2 * NT * NE], ones16, r_m16, start=True, stop=True).then_inc(s["cnt_ps"], 1)
            pe.wait_ge(s["cnt_done"], count(1))
            pe.wait_ge(s["b_zero"], count(1))

            def piece(sh, w, n, first):
                i, p, wd = PIECES[n]
                if not (first and n < 2):
                    pe.wait_ge(s["s1_done"], count(sh * NP_ + n - 1))
                t.matmul(PS[:, n % 2, 0:wd], q_st[w][0:3 * HD, i * P:(i + 1) * P], k_st[w][0:3 * HD, p * CH:p * CH + wd],
                         start=True, stop=True).then_inc(s["s1_ps"], 1)

            def max_row(sh, w, c, normed, bank, copied):
                pe.wait_ge(s["mx_done"], count((sh * NC + c + 1) * 2))
                pe.wait_ge(s["ot_done"], count(copied))
                pe.wait_ge(s["norm_done"], count(normed))
                pe.wait_ge(s["m_done"], count(sh * NC + c))
                for r in range(CT):
                    last = t.matmul(PS[3 * HD:3 * HD + 1, bank, r * P:(r + 1) * P], mx16[:, c, r:r + 1], ident16[:],
                                    start=True, stop=True)
                last.then_inc(s["m_ps"], 1)

            def heads(it, more, span):
                made = 0
                rows = 0
                for kk in span:
                    u, k = divmod(kk, NU)
                    if kk < 2 * NU or more:
                        c, j, wds, off, diag = UNITS[k]
                        pe.wait_ge(s["exp_done"], count(it * (2 * NU) + kk - 1))
                        if k in FIRST:
                            pe.wait_ge(s["m_done"], count((it * 2 + u) * NC + c + 1))
                        z = PS[:, 2 + 2 * (kk % 2):4 + 2 * (kk % 2), :].rearrange("p a s -> p (a s)")
                        beside = [(ahead, n) for ahead, n in slot_pieces(k) if u + ahead < 2 or more]
                        if k == S1_FROM and beside:
                            pe.wait_ge(s[f"ld{1 - u}"], count((it + 1 + u) * LOADS))
                        for a in range(2):
                            at = a * off
                            last = t.matmul(z[:, at:at + wds[a]], k_st[u % 2][0:3 * HD + 1, (j + a) * P:(j + a + 1) * P],
                                            q_st[u % 2][0:3 * HD + 1, (c + 1) * CH - wds[a]:(c + 1) * CH],
                                            start=True, stop=not diag)
                            if diag:
                                wm = 2 * P if (c, j, a) == (0, 0, 1) else P
                                last = t.matmul(z[:, at:at + wm], deny[:], later[:, int(wm > P), 0:wm], start=False, stop=True)
                            if a == 0 and beside:
                                ahead, n = beside[0]
                                piece(it * 2 + u + ahead, (u + ahead) % 2, n, False)
                        last.then_inc(s["s2_ps"], 1)
                    else:
                        beside = []
                    pk = kk - PV_LAG
                    piece_first = 0 <= pk and (pk < 2 * NU or more) and pk % NU in FIRST
                    if beside and piece_first:
                        ahead, n = beside[1]
                        piece(it * 2 + u + ahead, (u + ahead) % 2, n, False)
                    if 0 <= pk and (pk < 2 * NU or more):
                        pu, p_ = divmod(pk, NU)
                        c, j, wds, off, _m = UNITS[p_]
                        pe.wait_ge(s["exp_done"], count(it * (2 * NU) + pk + 1))
                        if p_ in FIRST:
                            pe.wait_ge(s["norm_done"], count(it * (2 * NC) + pu * NC + c - 1))
                            pe.wait_ge(s["m_done"], count(it * (2 * NC) + NC - 1 + rows))
                        for a in range(2):
                            rows_ = slice(2 * HD * a, 2 * HD * a + V1)
                            last = t.matmul(PS[rows_, 6 + c % 2, CH - wds[a]:CH], v_sb[pu % 2][:, j + a, :],
                                            probs[pk % 4][:, a * off:a * off + wds[a]],
                                            start=p_ in FIRST, stop=p_ in LAST)
                        last.then_inc(s["pv_done"], 1)
                    if beside and not piece_first:
                        ahead, n = beside[1]
                        piece(it * 2 + u + ahead, (u + ahead) % 2, n, False)
                    if kk < 2 * NU or more:
                        for ahead, cc in slot_max_rows(k):
                            if u + ahead < 2 or more:
                                max_row(it * 2 + u + ahead, (u + ahead) % 2, cc, it * (2 * NC) + made, free_bank(kk),
                                        it * (2 * NC) + (pk // NU) * NC + UNITS[pk % NU][0])
                                rows += 1
                    tk = kk - PV_LAG - 1
                    if tk >= 0 and tk % NU in LAST:
                        q = (tk // NU) * NC + LAST[tk % NU]
                        pe.wait_ge(s["ot_done"], count(it * (2 * NC) + q + 1))
                        pe.wait_ge(s["m_done"], count(it * (2 * NC) + NC - 1 + rows))
                        for r in range(CT):
                            W_ = 2 * HD + V1
                            last = t.transpose(PS[:, 6 + q % 2, r * W_:(r + 1) * W_], ot[q % 2][0:W_, r * P:(r + 1) * P], ident[0:W_, 0:W_])
                        last.then_inc(s["tr_ps"], 1)
                        made += 1

            LOADS = 7 * 16
            pe.wait_ge(s["ld0"], count(LOADS))
            for n in range(EARLY):
                piece(0, 0, n, True)
                if n in CHUNK_END:
                    max_row(0, 0, CHUNK_END[n], 0, 7, 0)
            heads(0, True, LEAD)
            with pe.Fori(0, BH // 2 - 1) as it:
                heads(it, True, SPAN)
            heads(BH // 2 - 1, False, SPAN)
            pe.wait_ge(s["norm_done"], count(NC * BH))

            def turn(n, i, q):
                u = q % 2
                pe.wait_ge(s[f"xg_in{q}"], (i + 1) * 16)
                pe.wait_ge(s["gT_done"], count(n - 1))
                for z in range(2):
                    for k in range(KB):
                        last = t.matmul(PS[:, 4 + 2 * u + z, k * P:(k + 1) * P], x_g[q][:, z * E + k * P:z * E + (k + 1) * P],
                                        ident16[:], start=True, stop=True)
                last.then_inc(s["gt_ps"], 1)

            pairs = ((0, 0), (1, 0), (0, 1))

            def experts(i, more):
                for q in range(AHEAD_G):
                    n, u = i * AHEAD_G + q, q % 2
                    if q < AHEAD_G - 1 or more:
                        turn(n + 1, i + (q + 1) // AHEAD_G, (q + 1) % AHEAD_G)
                    e = pe.value_load(expert_of[0:1, ds(n, 1)], min_val=0, max_val=NE - 1)
                    pe.wait_ge(s["gT_done"], count(n + 1))
                    pe.wait_ge(s["half_done"], count(n - 1))
                    terms = [(k, z, y) for k in range(KB) for z, y in pairs]
                    for q_, (k, z, y) in enumerate(terms):
                        w = (w_hi, w_lo)[y]
                        last = t.matmul(PS[:, u, :], xg_T[u][:, z, k, :],
                                        w[:, ds(e, 1), k * E:(k + 1) * E].rearrange("p e c -> p (e c)"),
                                        start=q_ == 0, stop=q_ == len(terms) - 1)
                    last.then_inc(s["z_ps"], 1)

            turn(0, 0, 0)
            with pe.Fori(0, PT // AHEAD_G - 1) as i:
                experts(i, True)
            experts(PT // AHEAD_G - 1, False)

            pe.wait_ge(s["gT_done"], count(PT))
            pe.wait_ge(s["half_done"], count(PT))

            def turn_heads(n, u):
                pe.wait_ge(s["o_lo_done"], count(n + 1))
                pe.wait_ge(s["oT_done"], count(n - 1))
                for z in range(2):
                    for k in range(KB):
                        last = t.matmul(PS[:, 4 + 2 * u + z, k * P:(k + 1) * P], o16[u][:, z, k * P:(k + 1) * P],
                                        ident16[:], start=True, stop=True)
                last.then_inc(s["otp_ps"], 1)

            def outs(i, more):
                for u in range(B):
                    n = i * B + u
                    if u == 0 or more:
                        turn_heads(n + 1, 1 - u)
                    pe.wait_ge(s["oT_done"], count(n + 1))
                    pe.wait_ge(s["acc_done"], count(n - 1))
                    terms = [(k, z, y) for k in range(KB) for z, y in pairs]
                    for q_, (k, z, y) in enumerate(terms):
                        last = t.matmul(PS[:, u, :], oT[u][:, z, k, :], comb_hl[:, y, k, :],
                                        start=q_ == 0, stop=q_ == len(terms) - 1)
                    last.then_inc(s["proj_ps"], 1)

            turn_heads(0, 0)
            with pe.Fori(0, ST - 1) as i:
                outs(i, True)
            outs(ST - 1, False)


_INS = ["x", "Wq", "Wdkv", "Wuk", "Wuv", "ln_g", "ln_b", "Wo_h", "Wo", "bo", "gate_w", "gate_b", "expert_w", "expert_b"]


def kernel(L0_attn_x, L0_attn_Wq, L0_attn_Wdkv, L0_attn_Wuk, L0_attn_Wuv, L0_attn_ln_g, L0_attn_ln_b, L0_attn_Wo_h,
           L0_attn_Wo, L0_attn_bo, L0_ffn_gate_w, L0_ffn_gate_b, L0_ffn_expert_w, L0_ffn_expert_b):
    import numpy as _np
    import concourse.bacc as _bacc
    from concourse import mybir as _mybir
    from concourse.bass_utils import run_bass_kernel_spmd as _run

    given = [L0_attn_x, L0_attn_Wq, L0_attn_Wdkv, L0_attn_Wuk, L0_attn_Wuv, L0_attn_ln_g, L0_attn_ln_b, L0_attn_Wo_h,
             L0_attn_Wo, L0_attn_bo, L0_ffn_gate_w, L0_ffn_gate_b, L0_ffn_expert_w, L0_ffn_expert_b]
    nc = _bacc.Bacc("TRN2", target_bir_lowering=False, num_devices=1)
    arrays, args = {}, []
    for name, value in zip(_INS, given):
        a = _np.ascontiguousarray(value)
        arrays[f"in_{name}"] = a
        args.append(nc.dram_tensor(f"in_{name}", a.shape, _mybir.dt.from_np(a.dtype), kind="ExternalInput").ap())
    out = nc.dram_tensor("out_0", tuple(L0_attn_x.shape), _mybir.dt.float32, kind="ExternalOutput").ap()
    layer_kernel(nc, *args, out)
    r = _run(nc, [arrays], core_ids=[0])
    return r.results[0]["out_0"]
```
